# Optimizing a Trainium2 kernel written in Bass

```python
import numpy as np
import jax
import jax.numpy as jnp

def _softmax(x, axis=-1):
    return jax.nn.softmax(x, axis=axis)

def _gelu(x):
    return jax.nn.gelu(x, approximate=True)

def _silu(x):
    return jax.nn.silu(x)

def _sigmoid(x):
    return jax.nn.sigmoid(x)

def _layernorm(x, axis=-1, eps=1e-05):
    m = jnp.mean(x, axis=axis, keepdims=True)
    v = jnp.var(x, axis=axis, keepdims=True)
    return (x - m) / jnp.sqrt(v + eps)

def _scatter_add(tgt, idx, src, axis=0):
    return tgt.at[idx].add(src)

def _segment_sum(src, seg, n):
    return jax.ops.segment_sum(src, seg, n)
kernel_name = 'mk_recurrent_d1_jaxref_r4_306570'

def setup_inputs(seed: int=0):
    np.random.seed(seed)
    _w = jnp.asarray

    def _L0_attn_setup():
        import jax, jax.numpy as jnp
        import numpy as np
        D_MODEL = 256
        D_FF = 1024
        FFN_H = int(2 * D_FF / 3)
        B, S = (4, 1024)
        LN_EPS = 1e-05
        ATTN_EPS = 1e-06

        def layer_norm(x, g, b):
            mu = jnp.mean(x, axis=-1, keepdims=True)
            var = jnp.mean(jnp.square(x - mu), axis=-1, keepdims=True)
            return (x - mu) * jax.lax.rsqrt(var + LN_EPS) * g + b
        key = jax.random.key(seed)
        ks = jax.random.split(key, 16)
        s = 0.02
        return {'x': jax.random.normal(ks[0], (B, S, D_MODEL), dtype=jnp.float32), 'Wqkv': jax.random.normal(ks[1], (D_MODEL, 3 * D_MODEL), dtype=jnp.float32) * s, 'bqkv': jnp.zeros((3 * D_MODEL,), jnp.float32), 'Wg': jax.random.normal(ks[2], (D_MODEL, FFN_H), dtype=jnp.float32) * s, 'bg': jnp.zeros((FFN_H,), jnp.float32), 'Wu': jax.random.normal(ks[3], (D_MODEL, FFN_H), dtype=jnp.float32) * s, 'bu': jnp.zeros((FFN_H,), jnp.float32), 'Wd': jax.random.normal(ks[4], (FFN_H, D_MODEL), dtype=jnp.float32) * s, 'bd': jnp.zeros((D_MODEL,), jnp.float32), 'g1': jnp.ones((D_MODEL,), jnp.float32), 'b1': jnp.zeros((D_MODEL,), jnp.float32), 'g2': jnp.ones((D_MODEL,), jnp.float32), 'b2': jnp.zeros((D_MODEL,), jnp.float32)}
    _L0_attn_in = _L0_attn_setup()

    def _L0_ffn_setup():
        import jax, jax.numpy as jnp
        import numpy as np
        EPS = 1e-05

        @jax.custom_vjp
        def ste_quantize(w):
            scale = jnp.maximum(jnp.mean(jnp.abs(w)), EPS)
            return jnp.clip(jnp.round(w / scale), -1.0, 1.0)

        def _ste_fwd(w):
            return (ste_quantize(w), None)

        def _ste_bwd(_, g):
            return (g,)
        ste_quantize.defvjp(_ste_fwd, _ste_bwd)
        key = jax.random.key(seed)
        k1, k2 = jax.random.split(key)
        x = jax.random.normal(k1, (8, 2048, 256), dtype=jnp.float32)
        weight = jax.random.normal(k2, (256, 256), dtype=jnp.float32) * 0.02
        return {'x': x, 'weight': weight}
    _L0_ffn_in = _L0_ffn_setup()
    _d = {'L0_attn_x': _L0_attn_in['x'], 'L0_attn_Wqkv': _L0_attn_in['Wqkv'], 'L0_attn_bqkv': _L0_attn_in['bqkv'], 'L0_attn_Wg': _L0_attn_in['Wg'], 'L0_attn_bg': _L0_attn_in['bg'], 'L0_attn_Wu': _L0_attn_in['Wu'], 'L0_attn_bu': _L0_attn_in['bu'], 'L0_attn_Wd': _L0_attn_in['Wd'], 'L0_attn_bd': _L0_attn_in['bd'], 'L0_attn_g1': _L0_attn_in['g1'], 'L0_attn_b1': _L0_attn_in['b1'], 'L0_attn_g2': _L0_attn_in['g2'], 'L0_attn_b2': _L0_attn_in['b2'], 'L0_ffn_weight': _L0_ffn_in['weight']}
    _x0 = _d['L0_attn_x']
    _d['L0_attn_x'] = jax.random.normal(jax.random.fold_in(jax.random.key(seed), 1), (8, 2048, 256), dtype=_x0.dtype)
    del _x0
    return _d

def reference(L0_attn_x, L0_attn_Wqkv, L0_attn_bqkv, L0_attn_Wg, L0_attn_bg, L0_attn_Wu, L0_attn_bu, L0_attn_Wd, L0_attn_bd, L0_attn_g1, L0_attn_b1, L0_attn_g2, L0_attn_b2, L0_ffn_weight):

    def _L0_attn_ref(x, Wqkv, bqkv, Wg, bg, Wu, bu, Wd, bd, g1, b1, g2, b2):
        import jax, jax.numpy as jnp
        import numpy as np
        D_MODEL = 256
        D_FF = 1024
        FFN_H = int(2 * D_FF / 3)
        B, S = (4, 1024)
        LN_EPS = 1e-05
        ATTN_EPS = 1e-06

        def layer_norm(x, g, b):
            mu = jnp.mean(x, axis=-1, keepdims=True)
            var = jnp.mean(jnp.square(x - mu), axis=-1, keepdims=True)
            return (x - mu) * jax.lax.rsqrt(var + LN_EPS) * g + b
        qkv = jnp.einsum('bsd,de->bse', x, Wqkv) + bqkv
        q, k, v = jnp.split(qkv, 3, axis=-1)
        qp = jax.nn.elu(q) + 1.0
        kp = jax.nn.elu(k) + 1.0
        kv = jnp.einsum('bsd,bse->bde', kp, v)
        num = jnp.einsum('bsd,bde->bse', qp, kv)
        k_sum = jnp.sum(kp, axis=1)
        den = jnp.einsum('bsd,bd->bs', qp, k_sum)[..., None]
        attn = num / (den + ATTN_EPS)
        x = layer_norm(x + attn, g1, b1)
        gate = jnp.einsum('bsd,dh->bsh', x, Wg) + bg
        up = jnp.einsum('bsd,dh->bsh', x, Wu) + bu
        ffn = jnp.einsum('bsh,hd->bsd', jax.nn.silu(gate) * up, Wd) + bd
        return layer_norm(x + ffn, g2, b2)

    def _L0_ffn_ref(x, weight):
        import jax, jax.numpy as jnp
        import numpy as np
        EPS = 1e-05

        @jax.custom_vjp
        def ste_quantize(w):
            scale = jnp.maximum(jnp.mean(jnp.abs(w)), EPS)
            return jnp.clip(jnp.round(w / scale), -1.0, 1.0)

        def _ste_fwd(w):
            return (ste_quantize(w), None)

        def _ste_bwd(_, g):
            return (g,)
        ste_quantize.defvjp(_ste_fwd, _ste_bwd)
        w_ternary = ste_quantize(weight)
        scale = jnp.maximum(jnp.mean(jnp.abs(weight)), EPS)
        return jnp.einsum('bsi,oi->bso', x, w_ternary * scale)
    x = L0_attn_x
    xn = _layernorm(x, axis=-1)
    s = _L0_attn_ref(xn, L0_attn_Wqkv, L0_attn_bqkv, L0_attn_Wg, L0_attn_bg, L0_attn_Wu, L0_attn_bu, L0_attn_Wd, L0_attn_bd, L0_attn_g1, L0_attn_b1, L0_attn_g2, L0_attn_b2)
    g = _silu(_L0_ffn_ref(xn, L0_ffn_weight))
    x = x + s * g
    return x

_drawn_inputs = setup_inputs


def setup_inputs(seed=0):
    import zlib

    import numpy as np

    out = dict(_drawn_inputs(seed))
    spreads = {'L0_attn_bqkv': (0.0, 0.714),
     'L0_attn_bg': (0.0, 2.0),
     'L0_attn_bu': (0.0, 2.0),
     'L0_attn_bd': (0.0, 2.0),
     'L0_attn_g1': (1.0, 0.6),
     'L0_attn_b1': (0.0, 0.8),
     'L0_attn_g2': (1.0, 0.6),
     'L0_attn_b2': (0.0, 0.681)}
    factors = {'L0_attn_Wqkv': 53.608, 'L0_attn_Wg': 8.0, 'L0_attn_Wu': 8.0, 'L0_attn_Wd': 8.0}
    for name, (base, spread) in spreads.items():
        noise = np.random.default_rng([zlib.crc32(name.encode()), seed]).standard_normal(out[name].shape)
        drawn = base * np.exp(spread * noise) if base else spread * noise
        out[name] = jnp.asarray(drawn.astype(out[name].dtype))
    for name, factor in factors.items():
        out[name] = (out[name] * factor).astype(out[name].dtype)
    return out
```

```python
from contextlib import ExitStack

import concourse.bass as bass
from concourse import mybir

P = 128
D = 256
DC = D // P
H = 682
HF = H // P
HT = H - HF * P
HC = HF + 1
UT = 64
BATCH, SEQ = 8, 2048
TOK = 512
TILES = TOK // P
PAIRS = TILES // 2
GROUPS = BATCH * SEQ // TOK
GPB = SEQ // TOK
LEAD = GPB + 1
KVW = D + 2
LN_EPS = 1e-5
ATTN_EPS = 1e-6
SCALE_EPS = 1e-5
RING = 5
HRING = 3
KP = 4
SG = 3
RZ = 3
XT = LEAD


def filling(i):
    return i + 1 < 0


def schedule(i):
    a, q, f = i + LEAD, i + 1, i
    jobs = []

    def add(kind, g, *idx):
        if 0 <= g < GROUPS:
            jobs.extend((kind, g, n) for n in idx)

    if a == 0:
        add("TX", 0, 0, 1)
    if filling(i):
        add("K", a, 0, 1, 2, 3)
        add("TX", a + 1, 0, 1)
        add("XK", a, 0, 1, 2, 3)
        return jobs
    add("Q", q, 0, 1)
    add("D", f - 1, 4)
    add("K", a, 0, 1)
    add("D", f - 1, 5)
    add("K", a, 2, 3)
    if q % GPB == 0:
        add("KV", q, 0, 1)
    add("G", f, 0)
    add("U", f, 0)
    add("N", q, 0)
    add("G", f, 1)
    add("U", f, 1)
    add("N", q, 1)
    add("B", q, 0)
    add("XK", a, 0)
    add("N", q, 2)
    add("G", f, 2)
    add("U", f, 2)
    add("D", f, 0)
    add("N", q, 3)
    add("B", q, 1)
    add("XK", a, 1)
    add("G", f, 3)
    add("U", f, 3)
    add("D", f, 1)
    add("XK", a, 2)
    add("TX", a + 1, 0)
    add("G", f, 4)
    add("U", f, 4)
    add("D", f, 2)
    add("XK", a, 3)
    add("TX", a + 1, 1)
    add("GU", f, 5)
    add("D", f, 3)
    add("TZ", q, 0, 1)
    return jobs


VECTORS = 11
ITERATIONS = range(-LEAD, GROUPS + 1)
OWN_BANK = ("D", "XK")
JOBS = [j for i in ITERATIONS for j in schedule(i) if j[0] not in OWN_BANK]
NUMBER = {j: n for n, j in enumerate(JOBS)}


def build_kernel(nc, x, wqkv, bqkv, wg, bg, wu, bu, wd, bd, g1, b1, g2, b2, wt, out):
    f32, f32r = mybir.dt.float32, mybir.dt.float32r
    ALU, ACT = mybir.AluOpType, mybir.ActivationFunctionType

    x_v = x.rearrange("b s d -> (b s) d").rearrange("(g t p) d -> g p t d", t=TILES, p=P)
    out_v = out.rearrange("b s d -> (b s) d").rearrange("(g t p) d -> g p t d", t=TILES, p=P)

    def row(v):
        return v.rearrange("(a n) -> a n", a=1)

    ctx = ExitStack()
    with ctx:
        def sb(name, shape, dt=f32):
            return ctx.enter_context(nc.sbuf_tensor(name, shape, dt))

        def sem(name):
            return ctx.enter_context(nc.semaphore(name))

        ident = sb("ident", [P, P])
        ones = sb("ones", [P, P])
        ones_r = sb("ones_r", [P, P], f32r)
        neg_half = sb("neg_half", [P, 1])
        wqk_h = sb("wqk_h", [P, DC, 2 * D], f32r)
        wqk_l = sb("wqk_l", [P, DC, 2 * D], f32r)
        tern = sb("tern", [P, DC, D], f32r)
        NGU = (2 * HF + 1) * P
        wgu_h = sb("wgu_h", [P, DC, NGU], f32r)
        wgu_l = sb("wgu_l", [P, DC, NGU], f32r)
        wd_h = sb("wd_h", [P, HC, D], f32r)
        wd_l = sb("wd_l", [P, HC, D], f32r)
        wv = sb("wv", [P, DC, KVW])
        bv1 = sb("bv1", [P, KVW])
        bk_parts = sb("bk_parts", [P, D], f32r)
        bq = sb("bq", [P, DC])
        bq1 = sb("bq1", [P, DC])
        nbq = sb("nbq", [P, DC])
        g1c = sb("g1c", [P, DC])
        b1c = sb("b1c", [P, DC])
        hb = sb("hb", [P, 2 * HC])
        hb0 = sb("hb0", [P, 2 * HC])
        tscale = sb("tscale", [P, 4])
        g1b = sb("g1b", [P, D])
        g2b = sb("g2b", [P, D])
        b2b = sb("b2b", [P, D])
        xa = sb("xa", [P, 2, TILES, D])
        xn = sb("xn", [P, TILES, D])
        xn_h = sb("xn_h", [P, TILES, D], f32r)
        xn_l = sb("xn_l", [P, TILES, D], f32r)
        xT_h = sb("xT_h", [P, XT, DC, TOK], f32r)
        xT_l = sb("xT_l", [P, XT, DC, TOK], f32r)
        st = sb("st", [P, 3, TILES, 6])
        mv = sb("mv", [P, 3, TILES, 2])
        ve = sb("ve", [P, 3, TILES])
        rstd0 = sb("rstd0", [P, GROUPS, TILES])
        nmr0 = sb("nmr0", [P, GROUPS, TILES])
        kp = sb("kp", [P, KP, D])
        kp_h = sb("kp_h", [P, TILES, D], f32r)
        kp_l = sb("kp_l", [P, TILES, D], f32r)
        ksum = sb("ksum", [P, 2, D])
        kv_h = sb("kv_h", [P, DC, KVW], f32r)
        kv_l = sb("kv_l", [P, DC, KVW], f32r)
        xq = sb("xq", [P, 3, TILES, D])
        qp = sb("qp", [P, DC, TOK])
        qp_h = sb("qp_h", [P, DC, TOK], f32r)
        qp_l = sb("qp_l", [P, DC, TOK], f32r)
        den = sb("den", [P, 2, 2])
        rstd1 = sb("rstd1", [P, TILES])
        nmr1 = sb("nmr1", [P, TILES])
        rz = sb("rz", [P, RZ, TILES, D])
        zT_h = sb("zT_h", [P, DC, TOK], f32r)
        zT_l = sb("zT_l", [P, DC, TOK], f32r)
        sg = sb("sg", [P, SG, TILES, D])
        hs = sb("hs", [P, 2, TOK])
        h_h = sb("h_h", [P, HRING, TOK], f32r)
        h_l = sb("h_l", [P, HRING, TOK], f32r)
        ht = sb("ht", [P, TOK], f32r)
        rstd2 = sb("rstd2", [P, TILES])

        bank = [ctx.enter_context(nc.psum_tensor(f"bank{n}", [P, 512], f32)) for n in range(RING)]
        xk_bank = ctx.enter_context(nc.psum_tensor("xk_bank", [P, 512], f32))
        d_bank = [ctx.enter_context(nc.psum_tensor(f"d_bank{n}", [P, 512], f32)) for n in range(2)]

        s_w = {n: sem("s_load_" + n) for n in ("qk", "t", "bk", "gu", "d", "v")}
        s_clear = sem("s_clear")
        s_vec = sem("s_vec")
        s_xa = [sem(f"s_xa{n}") for n in range(2)]
        s_xq = [sem(f"s_xq{n}") for n in range(3)]
        s_out = [sem(f"s_out{n}") for n in range(RZ)]
        s_cst = sem("s_cst")
        names = ("w_ones w_bq1 w_bk w_bkh w_bkl w_bkm w_bkp w_qkh w_qkl w_abs w_sum w_scale w_half "
                 "w_neg w_tern w_ternT w_tern_r w_hb0 w_hb w_gu w_guh w_gul w_dh w_dl "
                 "bn0 ag0 ve0 rs0 xn nm0 xh xl TX xTh xTl K mK eK kp kph kpl ks XK xk KV kvh kvl "
                 "Q mQ eQ qp qph qpl N d1 d2 xr r bn1 ag1 ve1 rs1 nm1 z TZ zTh zTl zg B sg "
                 "G GU S h hh hl D r2 bn2 ag2 ve2 rs2 a b c o").split()
        S = {n: sem("s_" + n) for n in names}

        def parts3(hi_l, lo_l, hi_r, lo_r):
            return ((hi_l, hi_r), (lo_l, hi_r), (hi_l, lo_r))

        def job_bank(kind, g, n):
            return bank[NUMBER[kind, g, n] % RING]

        def freed(kind, g, n):
            return {
                "TX": ("xTl", PAIRS * g + n + 1), "K": ("kp", TILES * g + n + 1),
                "Q": ("qp", DC * g + n + 1), "KV": ("kvl", DC * (g // GPB) + n + 1),
                "N": ("r", TILES * g + n + 1), "TZ": ("zTl", PAIRS * g + n + 1),
                "B": ("sg", PAIRS * g + n + 1), "G": ("S", HC * g + n + 1),
                "U": ("h", HC * g + n + 1), "GU": ("h", HC * g + n + 1),
            }[kind]

        block = ctx.enter_context(nc.Block())

        xk = hs[:, 0, :].rearrange("p (c n) -> p c n", c=DC)
        raw_qk = qp
        raw_t = hs
        rz_row = rz[:, :, :, :].rearrange("p a t d -> p (a t d)")
        raw_gu = rz_row[:, 0:DC * 2 * HF * P].rearrange("p (c n) -> p c n", c=DC)
        raw_tail = rz_row[:, DC * 2 * HF * P:DC * NGU].rearrange("p (c n) -> p c n", c=DC)
        raw_d = sg[:, :, :, :].rearrange("p a t d -> p (a t) d")
        raw_bk, low_bk = raw_d[:, HC, :], raw_d[:, HC + 1, :]

        @block.sync
        def _(eng):
            def load_xa(g):
                if g >= 2:
                    eng.wait_ge(S["xn"], TILES * (g - 1))
                eng.dma_start(xa[:, g % 2, :, :], x_v[g]).then_inc(s_xa[g % 2], 16)

            def load_xq(g):
                if g >= 3:
                    eng.wait_ge(S["o"], TILES * (g - 2))
                eng.dma_start(xq[:, g % 3, :, :], x_v[g]).then_inc(s_xq[g % 3], 16)

            def rows(v):
                return v.rearrange("(c p) n -> p c n", p=P)

            load_xa(0)
            eng.dma_start(raw_qk[:, :, :], rows(wqkv[:, 0:2 * D])).then_inc(s_w["qk"], 16)
            eng.dma_start(raw_t[:, :, 0:D], rows(wt)).then_inc(s_w["t"], 16)
            eng.dma_start(raw_bk, row(bqkv[D:2 * D]).to_broadcast([P, D])).then_inc(s_w["bk"], 16)
            load_xa(1)
            eng.wait_ge(s_clear, 3)
            for dst, v in ((bv1[:, 0:D], bqkv[2 * D:3 * D]), (g1b[:, :], g1), (g2b[:, :], g2), (b2b[:, :], b2)):
                eng.dma_start(dst, row(v).to_broadcast([P, D])).then_inc(s_vec, 16)
            with nc.allow_non_contiguous_dma(reason="a few vectors as columns"):
                for dst, v in ((bq[:, :], bqkv[0:D]), (g1c[:, :], g1), (b1c[:, :], b1)):
                    eng.dma_start(dst, v.rearrange("(c p) -> p c", p=P)).then_inc(s_vec, 16)
                for at, v in ((0, bg), (HC, bu)):
                    eng.dma_start(hb0[:, at:at + HF], v[0:HF * P].rearrange("(c p) -> p c", p=P)).then_inc(s_vec, 16)
                    eng.dma_start(hb0[0:HT, at + HF:at + HC],
                                  v[HF * P:H].rearrange("(c p) -> p c", c=1)).then_inc(s_vec, 16)
            eng.dma_start(raw_gu[:, :, 0:HF * P], rows(wg[:, 0:HF * P])).then_inc(s_w["gu"], 16)
            eng.dma_start(raw_gu[:, :, HF * P:2 * HF * P], rows(wu[:, 0:HF * P])).then_inc(s_w["gu"], 16)
            eng.dma_start(raw_tail[:, :, 0:HT], rows(wg[:, HF * P:H])).then_inc(s_w["gu"], 16)
            eng.dma_start(raw_tail[:, :, UT:UT + HT], rows(wu[:, HF * P:H])).then_inc(s_w["gu"], 16)
            eng.dma_start(raw_d[:, 0:HF, :], rows(wd[0:HF * P, :])).then_inc(s_w["d"], 16)
            for at in (0, UT):
                eng.dma_start(raw_d[at:at + HT, HF, :], wd[HF * P:H, :]).then_inc(s_w["d"], 16)
            eng.dma_start(raw_d[HT:HT + 1, HF, :], row(bd)).then_inc(s_w["d"], 16)
            eng.dma_start(raw_d[HT + 1:HT + 2, HF, :], row(b1)).then_inc(s_w["d"], 16)
            eng.dma_start(wv[:, :, 0:D], rows(wqkv[:, 2 * D:3 * D])).then_inc(s_w["v"], 16)
            for g in range(3):
                load_xq(g)

            for i in ITERATIONS:
                a, q, last = i + LEAD, i + 1, i - 1
                if a + 2 < GROUPS:
                    load_xa(a + 2)
                if 0 <= last < GROUPS:
                    eng.wait_ge(S["o"], TILES * (last + 1))
                    eng.dma_start(out_v[last], rz[:, last % RZ, :, :]).then_inc(s_out[last % RZ], 16)
                if 3 <= q + 1 < GROUPS:
                    load_xq(q + 1)
            for n in range(RZ):
                eng.wait_ge(s_out[n], 16 * len(range(n, GROUPS, RZ)))

        @block.gpsimd
        def _(eng):
            eng.memset(hb0[:, :], 0.0).then_inc(s_clear, 1)
            eng.memset(raw_tail, 0.0).then_inc(s_clear, 1)
            eng.memset(raw_d[:, HF, :], 0.0).then_inc(s_clear, 1)
            eng.memset(ident[:, :], 0.0).then_inc(s_cst, 1)
            eng.memset(ones[:, :], 1.0).then_inc(s_cst, 1)
            eng.memset(neg_half[:, :], -0.5).then_inc(s_cst, 1)
            eng.memset(wv[:, :, D:KVW], 0.0).then_inc(s_cst, 1)
            eng.memset(bv1[:, D:D + 1], 1.0).then_inc(s_cst, 1)
            eng.memset(bv1[:, D + 1:KVW], 0.0).then_inc(s_cst, 1)
            eng.memset(ht[:, :].bitcast(f32), 1.0).then_inc(s_cst, 1)
            eng.wait_ge(s_cst, 7)
            eng.affine_select(out=ident[:, :], in_=ident[:, :], compare_op=ALU.not_equal, fill=1.0,
                              base=0, pattern=[[-1, P]], channel_multiplier=1).then_inc(s_cst, 1)
            def rstd(k, g, dst):
                eng.wait_ge(S[f"ve{k}"], g + 1)
                if k == 1:
                    eng.wait_ge(S["z"], TILES * g)
                if k == 2:
                    eng.wait_ge(S["b"], TILES * g)
                eng.tensor_tensor(dst, ve[:, k, :], neg_half[:, 0:1].to_broadcast([P, TILES]),
                                  ALU.pow).then_inc(S[f"rs{k}"], 1)

            def xn_low(g):
                for p in range(PAIRS):
                    eng.wait_ge(S["xh"], PAIRS * g + p + 1)
                    if g:
                        eng.wait_ge(S["XK"], TILES * g)
                    t = slice(2 * p, 2 * p + 2)
                    eng.tensor_tensor(xn_l[:, t, :], xn[:, t, :], xn_h[:, t, :].bitcast(f32),
                                      ALU.subtract).then_inc(S["xl"], 1)

            def sum_k(g, t):
                n, slot = TILES * g + t, (g // GPB) % 2
                eng.wait_ge(S["kp"], n + 1)
                if g % GPB == 0 and t == 0:
                    if g >= 2 * GPB:
                        eng.wait_ge(S["KV"], DC * (g // GPB - 1))
                    eng.tensor_copy(ksum[:, slot, :], kp[:, n % KP, :]).then_inc(S["ks"], 1)
                else:
                    eng.wait_ge(S["ks"], n)
                    eng.tensor_tensor(ksum[:, slot, :], ksum[:, slot, :], kp[:, n % KP, :],
                                      ALU.add).then_inc(S["ks"], 1)

            def result(g, t):
                n, row_ = TILES * g + t, rz[:, g % RZ, t, :]
                eng.wait_ge(S["b"], n + 1)
                eng.wait_ge(S["sg"], PAIRS * g + t // 2 + 1)
                eng.tensor_tensor(row_, row_, sg[:, g % SG, t, :], ALU.mult).then_inc(S["c"], 1)
                eng.wait_ge(S["c"], n + 1)
                eng.tensor_tensor(row_, row_, xq[:, g % 3, t, :], ALU.add).then_inc(S["o"], 1)

            def z_g1(g, t):
                row_ = rz[:, g % RZ, t, :]
                eng.wait_ge(S["TZ"], PAIRS * g + t // 2 + 1)
                eng.tensor_tensor(row_, row_, g1b[:, :], ALU.mult).then_inc(S["zg"], 1)

            rstd(0, 0, rstd0[:, 0, :])
            eng.wait_ge(s_vec, 16 * VECTORS)
            for i in ITERATIONS:
                a, q, f, last = i + LEAD, i + 1, i, i - 1
                on = lambda g: 0 <= g < GROUPS
                if on(a):
                    xn_low(a)
                if on(a + 1):
                    rstd(0, a + 1, rstd0[:, a + 1, :])
                if on(a):
                    for t in range(TILES):
                        sum_k(a, t)
                if on(last):
                    rstd(2, last, rstd2[:, :])
                if on(f):
                    for t in range(TILES):
                        z_g1(f, t)
                if on(q):
                    rstd(1, q, rstd1[:, :])
                if on(last):
                    for t in range(TILES):
                        result(last, t)

        @block.scalar
        def _(eng):
            def act(out_, in_, func, name, **kw):
                return eng.activation(out_, in_, func, **kw).then_inc(S[name], 1)

            def xn_high(g):
                for p in range(PAIRS):
                    t = slice(2 * p, 2 * p + 2)
                    eng.wait_ge(S["xn"], TILES * g + 2 * p + 2)
                    if g:
                        eng.wait_ge(S["XK"], TILES * g)
                    act(xn_h[:, t, :], xn[:, t, :], ACT.Copy, "xh")

            def xT_high(g, p):
                eng.wait_ge(S["TX"], PAIRS * g + p + 1)
                if g >= XT and p == 0:
                    eng.wait_ge(S["B"], PAIRS * (g - XT + 1))
                act(xT_h[:, g % XT, :, p * D:(p + 1) * D],
                    job_bank("TX", g, p)[:, :].rearrange("p (c n) -> p c n", c=DC), ACT.Copy, "xTh")

            def k_exp(g, t):
                n = TILES * g + t
                eng.wait_ge(S["K"], n + 1)
                if n >= KP:
                    eng.wait_ge(S["kpl"], n - KP + 1)
                    eng.wait_ge(S["ks"], n - KP + 1)
                act(kp[:, n % KP, :], job_bank("K", g, t)[:, 0:D], ACT.Relu, "mK", scale=-1.0, bias=ones[:, 0:1])
                eng.wait_ge(S["mK"], n + 1)
                act(kp[:, n % KP, :], kp[:, n % KP, :], ACT.Exp, "eK", scale=-1.0)

            def k_high(g, t):
                n = TILES * g + t
                eng.wait_ge(S["kp"], n + 1)
                if g:
                    eng.wait_ge(S["XK"], TILES * (g - 1) + t + 1)
                act(kp_h[:, t, :], kp[:, n % KP, :], ACT.Copy, "kph")

            def q_exp(g, c):
                eng.wait_ge(S["Q"], DC * g + c + 1)
                if g:
                    eng.wait_ge(S["qpl"], DC * (g - 1) + c + 1)
                if g == 0:
                    eng.wait_ge(S["w_bq1"], 2)
                act(qp[:, c, :], job_bank("Q", g, c)[:, :], ACT.Relu, "mQ", scale=-1.0, bias=nbq[:, c:c + 1])
                eng.wait_ge(S["mQ"], DC * g + c + 1)
                act(qp[:, c, :], qp[:, c, :], ACT.Exp, "eQ", scale=-1.0)

            def q_high(g, c):
                eng.wait_ge(S["qp"], DC * g + c + 1)
                if g:
                    eng.wait_ge(S["N"], TILES * g)
                act(qp_h[:, c, :], qp[:, c, :], ACT.Copy, "qph")

            def x_res(g, t):
                eng.wait_ge(s_xq[g % 3], 16 * (g // 3 + 1))
                eng.wait_ge(S["nm0"], g + 1)
                if g >= RZ and t == 0:
                    eng.wait_ge(s_out[g % RZ], 16 * (g // RZ))
                act(rz[:, g % RZ, t, :], xq[:, g % 3, t, :], ACT.Identity, "xr",
                    scale=rstd0[:, g, t:t + 1], bias=nmr0[:, g, t:t + 1])

            def z_rows(g, t):
                eng.wait_ge(S["nm1"], g + 1)
                act(rz[:, g % RZ, t, :], rz[:, g % RZ, t, :], ACT.Identity, "z",
                    scale=rstd1[:, t:t + 1], bias=nmr1[:, t:t + 1])

            def zT_high(g, p):
                eng.wait_ge(S["TZ"], PAIRS * g + p + 1)
                if g:
                    eng.wait_ge(S["GU"], g)
                act(zT_h[:, :, p * D:(p + 1) * D],
                    job_bank("TZ", g, p)[:, :].rearrange("p (c n) -> p c n", c=DC), ACT.Copy, "zTh")

            def silu_gate(g, c):
                n, rows = HC * g + c, P if c < HF else HT
                if c < HF:
                    eng.wait_ge(S["G"], 2 * (HF * g + c) + 1)
                    src = job_bank("G", g, c)
                else:
                    eng.wait_ge(S["GU"], g + 1)
                    src = job_bank("GU", g, c)
                if n >= 2:
                    eng.wait_ge(S["hl"], n - 1)
                if c == 0 and (g + 1) % GPB == 0 and g + 1 < GROUPS:
                    eng.wait_ge(S["KV"], DC * ((g + 1) // GPB + 1))
                act(hs[0:rows, n % 2, :], src[0:rows, :], ACT.Silu, "S", bias=hb[0:rows, c:c + 1])

            def h_high(g, c):
                n, rows = HC * g + c, P if c < HF else HT
                eng.wait_ge(S["h"], n + 1)
                if c < HF:
                    m = HF * g + c
                    if m >= HRING:
                        gb, cb = divmod(m - HRING, HF)
                        eng.wait_ge(S["D"], HC * gb + cb + 1)
                    dst = h_h[:, m % HRING, :]
                else:
                    if g:
                        eng.wait_ge(S["D"], HC * g)
                    dst = ht[0:rows, :]
                act(dst, hs[0:rows, n % 2, :], ACT.Copy, "hh")

            def silu_tern(g, p):
                eng.wait_ge(S["B"], PAIRS * g + p + 1)
                if g >= SG:
                    eng.wait_ge(S["c"], TILES * (g - SG) + 2 * p + 2)
                act(sg[:, g % SG, 2 * p:2 * p + 2, :],
                    job_bank("B", g, p)[:, :].rearrange("p (t n) -> p t n", t=2),
                    ACT.Silu, "sg", scale=tscale[:, 1:2])

            eng.wait_ge(s_w["qk"], 16)
            act(wqk_h[:, :, :], raw_qk[:, :, :], ACT.Copy, "w_qkh")
            eng.wait_ge(s_w["t"], 16)
            act(raw_t[:, :, D:2 * D], raw_t[:, :, 0:D], ACT.Abs, "w_abs", accum_out=tscale[:, 2:3])
            xn_high(0)
            xT_high(0, 0)
            xT_high(0, 1)

            for i in ITERATIONS:
                a, q, f = i + LEAD, i + 1, i
                on = lambda g: 0 <= g < GROUPS
                if i == 1 - LEAD:
                    eng.wait_ge(S["w_gu"], 2 * DC)
                    act(wgu_h[:, :, 0:2 * HF * P], raw_gu, ACT.Copy, "w_guh")
                    act(wgu_h[:, :, 2 * HF * P:NGU], raw_tail, ACT.Copy, "w_guh")
                    eng.wait_ge(s_w["d"], 16 * 5)
                    act(wd_h[:, :, :], raw_d[:, 0:HC, :], ACT.Copy, "w_dh")
                if filling(i):
                    k_exp(a, 0)
                    k_exp(a, 1)
                    k_high(a, 0)
                    k_exp(a, 2)
                    k_high(a, 1)
                    k_exp(a, 3)
                    k_high(a, 2)
                    k_high(a, 3)
                    xT_high(a + 1, 0)
                    xT_high(a + 1, 1)
                    xn_high(a + 1)
                    continue
                if on(f):
                    zT_high(f, 0)
                if on(q) and q % GPB == 0:
                    eng.wait_ge(S["XK"], TILES * (q + GPB))
                    if q:
                        eng.wait_ge(S["KV"], DC * (q // GPB))
                        eng.wait_ge(S["hl"], HC * f)
                    act(xk, xk_bank[:, :].rearrange("p (c n) -> p c n", c=DC), ACT.Copy, "xk")
                if on(q):
                    q_exp(q, 0)
                if on(f):
                    zT_high(f, 1)
                if on(q):
                    q_exp(q, 1)
                if on(a):
                    k_exp(a, 0)
                if on(q):
                    q_high(q, 0)
                if on(a):
                    k_exp(a, 1)
                    k_high(a, 0)
                if on(q):
                    q_high(q, 1)
                if on(a):
                    k_exp(a, 2)
                    k_high(a, 1)
                    k_exp(a, 3)
                    k_high(a, 2)
                    k_high(a, 3)
                if on(q) and q % GPB == 0:
                    for c in range(DC):
                        eng.wait_ge(S["KV"], DC * (q // GPB) + c + 1)
                        if c == 0 and q:
                            eng.wait_ge(S["N"], TILES * q)
                        act(kv_h[:, c, :], job_bank("KV", q, c)[:, 0:KVW], ACT.Copy, "kvh")
                if on(f):
                    silu_gate(f, 0)
                if on(q):
                    x_res(q, 0)
                    x_res(q, 1)
                if on(f):
                    h_high(f, 0)
                    silu_gate(f, 1)
                if on(q):
                    x_res(q, 2)
                    x_res(q, 3)
                if on(f):
                    h_high(f, 1)
                if on(q):
                    silu_tern(q, 0)
                if on(f):
                    silu_gate(f, 2)
                    h_high(f, 2)
                if on(q):
                    silu_tern(q, 1)
                if on(f):
                    silu_gate(f, 3)
                    h_high(f, 3)
                if on(a + 1):
                    xT_high(a + 1, 0)
                if on(q):
                    for t in range(TILES):
                        z_rows(q, t)
                if on(f):
                    silu_gate(f, 4)
                    h_high(f, 4)
                if on(a + 1):
                    xT_high(a + 1, 1)
                if on(f):
                    silu_gate(f, 5)
                    h_high(f, 5)
                if on(a + 1):
                    xn_high(a + 1)

        @block.vector
        def _(eng):
            def stats(k, g, t, rows):
                n = TILES * g + t
                if n >= TILES:
                    eng.wait_ge(S[f"ag{k}"], n - TILES + 1)
                eng.bn_stats(st[:, k, t, :], rows).then_inc(S[f"bn{k}"], 1)

            def aggregate(k, g):
                for t in range(TILES):
                    eng.wait_ge(S[f"bn{k}"], TILES * g + t + 1)
                    if g and t == 0:
                        eng.wait_ge(S[{0: "nm0", 1: "nm1", 2: "a"}[k]], {0: g, 1: g, 2: TILES * g}[k])
                    eng.bn_aggr(mv[:, k, t, :], st[:, k, t, :]).then_inc(S[f"ag{k}"], 1)
                eng.wait_ge(S[f"ag{k}"], TILES * (g + 1))
                if g:
                    eng.wait_ge(S[f"rs{k}"], g)
                eng.tensor_scalar(ve[:, k, :], mv[:, k, :, 1], LN_EPS, None, ALU.add)\
                   .then_inc(S[f"ve{k}"], 1)

            def a_stats(g):
                eng.wait_ge(s_xa[g % 2], 16 * (g // 2 + 1))
                for t in range(TILES):
                    stats(0, g, t, xa[:, g % 2, t, :])
                aggregate(0, g)

            def a_norm(g):
                eng.wait_ge(S["rs0"], g + 1)
                if g:
                    eng.wait_ge(S["xl"], PAIRS * g)
                    eng.wait_ge(S["TX"], PAIRS * g)
                for t in range(TILES):
                    eng.tensor_scalar(xn[:, t, :], xa[:, g % 2, t, :], mv[:, 0, t, 0:1],
                                      rstd0[:, g, t:t + 1], ALU.subtract, ALU.mult).then_inc(S["xn"], 1)
                eng.scalar_tensor_tensor(out=nmr0[:, g, :], in0=mv[:, 0, :, 0], scalar=-1.0,
                                         in1=rstd0[:, g, :], op0=ALU.mult, op1=ALU.mult).then_inc(S["nm0"], 1)

            def xT_low(g, p):
                eng.wait_ge(S["xTh"], PAIRS * g + p + 1)
                cols = slice(p * D, (p + 1) * D)
                eng.tensor_tensor(xT_l[:, g % XT, :, cols],
                                  job_bank("TX", g, p)[:, :].rearrange("p (c n) -> p c n", c=DC),
                                  xT_h[:, g % XT, :, cols].bitcast(f32), ALU.subtract).then_inc(S["xTl"], 1)

            def k_elu(g, t):
                n = TILES * g + t
                eng.wait_ge(S["eK"], n + 1)
                eng.tensor_tensor(kp[:, n % KP, :], job_bank("K", g, t)[:, 0:D], kp[:, n % KP, :],
                                  ALU.max).then_inc(S["kp"], 1)

            def k_low(g, t):
                n = TILES * g + t
                eng.wait_ge(S["kph"], n + 1)
                eng.tensor_tensor(kp_l[:, t, :], kp[:, n % KP, :], kp_h[:, t, :].bitcast(f32),
                                  ALU.subtract).then_inc(S["kpl"], 1)

            def q_elu(g, c):
                n = DC * g + c
                eng.wait_ge(S["eQ"], n + 1)
                eng.scalar_tensor_tensor(out=qp[:, c, :], in0=job_bank("Q", g, c)[:, :],
                                         scalar=bq1[:, c:c + 1], in1=qp[:, c, :],
                                         op0=ALU.add, op1=ALU.max).then_inc(S["qp"], 1)

            def q_low(g, c):
                eng.wait_ge(S["qph"], DC * g + c + 1)
                eng.tensor_tensor(qp_l[:, c, :], qp[:, c, :], qp_h[:, c, :].bitcast(f32),
                                  ALU.subtract).then_inc(S["qpl"], 1)

            def attn(g, t):
                n, num = TILES * g + t, job_bank("N", g, t)
                eng.wait_ge(S["N"], n + 1)
                eng.tensor_scalar(den[:, n % 2, 0:1], num[:, D:D + 1], ATTN_EPS, None, ALU.add)\
                   .then_inc(S["d1"], 1)
                eng.wait_ge(S["d1"], n + 1)
                eng.reciprocal(den[:, n % 2, 1:2], den[:, n % 2, 0:1]).then_inc(S["d2"], 1)
                eng.wait_ge(S["d2"], n + 1)
                eng.wait_ge(S["xr"], n + 1)
                eng.scalar_tensor_tensor(out=rz[:, g % RZ, t, :], in0=num[:, 0:D],
                                         scalar=den[:, n % 2, 1:2], in1=rz[:, g % RZ, t, :],
                                         op0=ALU.mult, op1=ALU.add).then_inc(S["r"], 1)
                eng.wait_ge(S["r"], n + 1)
                stats(1, g, t, rz[:, g % RZ, t, :])

            def attn_norm(g):
                eng.wait_ge(S["rs1"], g + 1)
                if g:
                    eng.wait_ge(S["z"], TILES * g)
                eng.scalar_tensor_tensor(out=nmr1[:, :], in0=mv[:, 1, :, 0], scalar=-1.0,
                                         in1=rstd1[:, :], op0=ALU.mult, op1=ALU.mult).then_inc(S["nm1"], 1)

            def zT_low(g, p):
                eng.wait_ge(S["zTh"], PAIRS * g + p + 1)
                cols = slice(p * D, (p + 1) * D)
                eng.tensor_tensor(zT_l[:, :, cols],
                                  job_bank("TZ", g, p)[:, :].rearrange("p (c n) -> p c n", c=DC),
                                  zT_h[:, :, cols].bitcast(f32), ALU.subtract).then_inc(S["zTl"], 1)

            def h_rows(g, c):
                n, rows = HC * g + c, P if c < HF else HT
                if c < HF:
                    eng.wait_ge(S["G"], 2 * (HF * g + c + 1))
                    up = job_bank("U", g, c)[:, :]
                else:
                    up = job_bank("GU", g, c)[UT:UT + HT, :]
                eng.wait_ge(S["S"], n + 1)
                eng.scalar_tensor_tensor(out=hs[0:rows, n % 2, :], in0=up,
                                         scalar=hb[0:rows, HC + c:HC + c + 1],
                                         in1=hs[0:rows, n % 2, :], op0=ALU.add, op1=ALU.mult)\
                   .then_inc(S["h"], 1)

            def h_low(g, c):
                n, rows = HC * g + c, P if c < HF else HT
                eng.wait_ge(S["hh"], n + 1)
                hi, lo = ((h_h[:, (HF * g + c) % HRING, :], h_l[:, (HF * g + c) % HRING, :]) if c < HF
                          else (ht[0:rows, :], ht[UT:UT + rows, :]))
                eng.tensor_tensor(lo, hs[0:rows, n % 2, :], hi.bitcast(f32),
                                  ALU.subtract).then_inc(S["hl"], 1)

            def ffn_rows(g):
                eng.wait_ge(S["D"], HC * (g + 1))
                for t in range(TILES):
                    eng.wait_ge(S["zg"], TILES * g + t + 1)
                    row_ = rz[:, g % RZ, t, :]
                    eng.tensor_tensor(row_, d_bank[t // 2][:, (t % 2) * D:(t % 2 + 1) * D], row_,
                                      ALU.add).then_inc(S["r2"], 1)

            def last_stats(g):
                for t in range(TILES):
                    eng.wait_ge(S["r2"], TILES * g + t + 1)
                    stats(2, g, t, rz[:, g % RZ, t, :])
                aggregate(2, g)

            def last_norm(g, p):
                eng.wait_ge(S["rs2"], g + 1)
                pair = range(2 * p, 2 * p + 2)
                for t in pair:
                    row_ = rz[:, g % RZ, t, :]
                    eng.scalar_tensor_tensor(out=row_, in0=row_, scalar=mv[:, 2, t, 0:1], in1=g2b[:, :],
                                             op0=ALU.subtract, op1=ALU.mult).then_inc(S["a"], 1)
                for t in pair:
                    row_ = rz[:, g % RZ, t, :]
                    eng.wait_ge(S["a"], TILES * g + t + 1)
                    eng.scalar_tensor_tensor(out=row_, in0=row_, scalar=rstd2[:, t:t + 1], in1=b2b[:, :],
                                             op0=ALU.mult, op1=ALU.add).then_inc(S["b"], 1)

            def kv_low(g, c):
                eng.wait_ge(S["kvh"], DC * (g // GPB) + c + 1)
                eng.tensor_tensor(kv_l[:, c, :], job_bank("KV", g, c)[:, 0:KVW],
                                  kv_h[:, c, :].bitcast(f32), ALU.subtract).then_inc(S["kvl"], 1)

            def setup_k():
                eng.wait_ge(s_cst, 8)
                eng.tensor_copy(ones_r[:, :], ones[:, :]).then_inc(S["w_ones"], 1)
                eng.wait_ge(S["w_qkh"], 1)
                eng.tensor_tensor(wqk_l[:, :, :], raw_qk[:, :, :], wqk_h[:, :, :].bitcast(f32),
                                  ALU.subtract).then_inc(S["w_qkl"], 1)
                eng.wait_ge(s_vec, 16 * VECTORS)
                eng.tensor_scalar(bq1[:, :], bq[:, :], 1.0, None, ALU.add).then_inc(S["w_bq1"], 1)
                eng.tensor_scalar(nbq[:, :], bq[:, :], -1.0, None, ALU.mult).then_inc(S["w_bq1"], 1)
                eng.wait_ge(s_w["bk"], 16)
                eng.tensor_scalar(raw_bk, raw_bk, 1.0, None, ALU.add).then_inc(S["w_bk"], 1)
                eng.wait_ge(S["w_bk"], 1)
                eng.tensor_copy(bk_parts[:, :], raw_bk).then_inc(S["w_bkh"], 1)
                eng.wait_ge(S["w_bkh"], 1)
                eng.tensor_tensor(low_bk, raw_bk, bk_parts[:, :].bitcast(f32), ALU.subtract)\
                   .then_inc(S["w_bkl"], 1)
                eng.wait_ge(S["w_bkl"], 1)
                eng.tensor_scalar(low_bk, low_bk, ident[:, 1:2], None, ALU.mult).then_inc(S["w_bkm"], 1)
                eng.wait_ge(S["w_bkm"], 1)
                eng.scalar_tensor_tensor(out=bk_parts[:, :], in0=bk_parts[:, :].bitcast(f32),
                                         scalar=ident[:, 0:1], in1=low_bk,
                                         op0=ALU.mult, op1=ALU.add).then_inc(S["w_bkp"], 1)

            def setup_ternary():
                eng.wait_ge(S["w_sum"], 1)
                eng.tensor_scalar(tscale[:, 1:2], d_bank[0][:, 0:1], 1.0 / (D * D), SCALE_EPS,
                                  ALU.mult, ALU.max).then_inc(S["w_scale"], 1)
                eng.wait_ge(S["w_scale"], 1)
                eng.tensor_scalar(tscale[:, 0:1], tscale[:, 1:2], 0.5, None, ALU.mult)\
                   .then_inc(S["w_half"], 1)
                eng.wait_ge(S["w_half"], 1)
                eng.tensor_scalar(raw_t[:, :, D:2 * D], raw_t[:, :, 0:D], -1.0, tscale[:, 0:1],
                                  ALU.mult, ALU.is_gt).then_inc(S["w_neg"], 1)
                eng.wait_ge(S["w_neg"], 1)
                eng.scalar_tensor_tensor(out=raw_t[:, :, 0:D], in0=raw_t[:, :, 0:D], scalar=tscale[:, 0:1],
                                         in1=raw_t[:, :, D:2 * D], op0=ALU.is_gt, op1=ALU.subtract)\
                   .then_inc(S["w_tern"], 1)
                eng.wait_ge(S["w_ternT"], 1)
                eng.tensor_copy(tern[:, :, :], d_bank[1][:, :].rearrange("p (c n) -> p c n", c=DC))\
                   .then_inc(S["w_tern_r"], 1)

            def setup_gate_up():
                eng.wait_ge(S["w_hb0"], 1)
                eng.tensor_tensor(cols(hb)[:, :, 0:HF], cols(d_bank[0])[:, :, 0:HF],
                                  cols(hb0)[:, :, 0:HF], ALU.add).then_inc(S["w_hb"], 1)
                eng.tensor_tensor(cols(hb)[0:HT, :, HF:HC], cols(d_bank[0])[0:HT, :, HF:HC],
                                  cols(hb0)[0:HT, :, HF:HC], ALU.add).then_inc(S["w_hb"], 1)
                for c in range(DC):
                    for raw in (raw_gu, raw_tail):
                        eng.tensor_scalar(raw[:, c, :], raw[:, c, :], g1c[:, c:c + 1], None, ALU.mult)\
                           .then_inc(S["w_gu"], 1)

            def setup_low():
                eng.wait_ge(S["w_guh"], 2)
                eng.tensor_tensor(wgu_l[:, :, 0:2 * HF * P], raw_gu,
                                  wgu_h[:, :, 0:2 * HF * P].bitcast(f32), ALU.subtract).then_inc(S["w_gul"], 1)
                eng.tensor_tensor(wgu_l[:, :, 2 * HF * P:NGU], raw_tail,
                                  wgu_h[:, :, 2 * HF * P:NGU].bitcast(f32), ALU.subtract).then_inc(S["w_gul"], 1)
                eng.wait_ge(S["w_dh"], 1)
                eng.memset(wd_l[UT:P, HF, :].bitcast(f32), 0.0).then_inc(S["w_dl"], 1)
                for rows, c in ((P, slice(0, HF)), (UT, slice(HF, HC))):
                    eng.tensor_tensor(wd_l[0:rows, c, :], raw_d[0:rows, c, :], wd_h[0:rows, c, :].bitcast(f32),
                                      ALU.subtract).then_inc(S["w_dl"], 1)

            def cols(t):
                return t[:, 0:2 * HC].rearrange("p (a c) -> p a c", a=2)

            def setups(i):
                if i == -LEAD:
                    setup_gate_up()
                if i == 1 - LEAD:
                    setup_low()
                if i == 2 - LEAD:
                    setup_ternary()

            a_stats(0)
            a_norm(0)
            setup_k()
            xT_low(0, 0)
            xT_low(0, 1)

            for i in ITERATIONS:
                a, q, f, last = i + LEAD, i + 1, i, i - 1
                on = lambda g: 0 <= g < GROUPS
                if filling(i):
                    a_stats(a + 1)
                    k_elu(a, 0)
                    k_elu(a, 1)
                    k_low(a, 0)
                    a_norm(a + 1)
                    k_elu(a, 2)
                    k_low(a, 1)
                    k_elu(a, 3)
                    k_low(a, 2)
                    xT_low(a + 1, 0)
                    k_low(a, 3)
                    xT_low(a + 1, 1)
                    setups(i)
                    continue
                if on(f):
                    zT_low(f, 0)
                if on(a + 1):
                    a_stats(a + 1)
                if on(q):
                    q_elu(q, 0)
                if on(f):
                    zT_low(f, 1)
                if on(q):
                    q_elu(q, 1)
                    q_low(q, 0)
                if on(a):
                    k_elu(a, 0)
                if on(q):
                    q_low(q, 1)
                if on(a):
                    k_elu(a, 1)
                    k_low(a, 0)
                    k_elu(a, 2)
                    k_low(a, 1)
                    k_elu(a, 3)
                    k_low(a, 2)
                if on(a + 1):
                    a_norm(a + 1)
                if on(a):
                    k_low(a, 3)
                if on(q) and q % GPB == 0:
                    kv_low(q, 0)
                    kv_low(q, 1)
                if on(last):
                    ffn_rows(last)
                if on(f):
                    h_rows(f, 0)
                if on(q):
                    attn(q, 0)
                if on(f):
                    h_low(f, 0)
                if on(last):
                    last_stats(last)
                if on(f):
                    h_rows(f, 1)
                if on(q):
                    attn(q, 1)
                if on(f):
                    h_low(f, 1)
                if on(q):
                    attn(q, 2)
                if on(f):
                    h_rows(f, 2)
                if on(q):
                    attn(q, 3)
                if on(f):
                    h_low(f, 2)
                if on(q):
                    aggregate(1, q)
                if on(f):
                    h_rows(f, 3)
                    h_low(f, 3)
                if on(q):
                    attn_norm(q)
                if on(last):
                    last_norm(last, 0)
                if on(a + 1):
                    xT_low(a + 1, 0)
                if on(last):
                    last_norm(last, 1)
                if on(f):
                    h_rows(f, 4)
                    h_low(f, 4)
                if on(a + 1):
                    xT_low(a + 1, 1)
                if on(f):
                    h_rows(f, 5)
                    h_low(f, 5)

        @block.tensor
        def _(eng):
            def products(dst, pairs, name, first=True, last=True, **kw):
                for n, (left, right) in enumerate(pairs):
                    ins = eng.matmul(dst, left, right, start=first and n == 0,
                                     stop=last and n == len(pairs) - 1, **kw)
                if name:
                    ins.then_inc(S[name], 1)

            def x_parts(g, t):
                s = slice(t * P, (t + 1) * P)
                return [(xT_h[:, g % XT, c, s], xT_l[:, g % XT, c, s]) for c in range(DC)]

            def transposes(dst, src, p, name):
                for c in range(DC):
                    for t in range(2):
                        ins = eng.transpose(dst[:, c * D + t * P:c * D + (t + 1) * P],
                                            src[:, 2 * p + t, c * P:(c + 1) * P], ident[:, :])
                ins.then_inc(S[name], 1)

            def TX(g, p, dst):
                eng.wait_ge(S["xn"], TILES * g + 2 * p + 2)
                transposes(dst, xn, p, "TX")

            def TZ(g, p, dst):
                eng.wait_ge(S["z"], TILES * g + 2 * p + 2)
                transposes(dst, rz[:, g % RZ, :, :], p, "TZ")

            def K(g, t, dst):
                eng.wait_ge(S["xTl"], PAIRS * g + t // 2 + 1)
                if g == 0 and t == 0:
                    eng.wait_ge(S["w_qkl"], 1)
                    eng.wait_ge(S["w_bkp"], 1)
                w = slice(D, 2 * D)
                products(dst[:, 0:D], [(ones_r[:, :], bk_parts[:, :])] + [
                    pair for c, (xh, xl) in enumerate(x_parts(g, t))
                    for pair in parts3(xh, xl, wqk_h[:, c, w], wqk_l[:, c, w])], "K")

            def B(g, p, dst):
                if g == 0 and p == 0:
                    eng.wait_ge(S["w_tern_r"], 1)
                for t in range(2):
                    products(dst[:, t * D:(t + 1) * D],
                             [(part, tern[:, c, :]) for c, parts in enumerate(x_parts(g, 2 * p + t))
                              for part in parts], "B" if t else None)

            def Q(g, c, dst):
                eng.wait_ge(S["xTl"], PAIRS * (g + 1))
                w = slice(c * P, (c + 1) * P)
                products(dst[:, :], [
                    pair for k in range(DC)
                    for pair in parts3(wqk_h[:, k, w], wqk_l[:, k, w],
                                       xT_h[:, g % XT, k, :], xT_l[:, g % XT, k, :])], "Q")

            def XK(g, t):
                n, of = TILES * (g % GPB) + t, TILES * GPB
                eng.wait_ge(S["kpl"], TILES * g + t + 1)
                eng.wait_ge(S["xl"], PAIRS * g + t // 2 + 1)
                if n == 0:
                    eng.wait_ge(S["xk"], g // GPB)
                for c in range(DC):
                    w = slice(c * P, (c + 1) * P)
                    products(xk_bank[:, c * D:(c + 1) * D],
                             parts3(xn_h[:, t, w], xn_l[:, t, w], kp_h[:, t, :], kp_l[:, t, :]),
                             "XK" if c == DC - 1 else None, first=n == 0 and c == 0,
                             last=n == of - 1, skip_group_check=True)

            def KV(g, c, dst):
                batch = g // GPB
                eng.wait_ge(S["xk"], batch + 1)
                eng.wait_ge(S["ks"], TILES * (g + GPB))
                if g == 0:
                    eng.wait_ge(s_w["v"], 16)
                    eng.wait_ge(s_vec, 16 * VECTORS)
                    eng.wait_ge(s_cst, 8)
                w = slice(c * P, (c + 1) * P)
                products(dst[:, 0:KVW], [(xk[:, k, w], wv[:, k, :]) for k in range(DC)]
                         + [(ksum[:, batch % 2, w], bv1[:, :])], "KV")

            def N(g, t, dst):
                eng.wait_ge(S["qpl"], DC * (g + 1))
                eng.wait_ge(S["kvl"], DC * (g // GPB + 1))
                s = slice(t * P, (t + 1) * P)
                products(dst[:, 0:KVW], [
                    pair for c in range(DC)
                    for pair in parts3(qp_h[:, c, s], qp_l[:, c, s], kv_h[:, c, :], kv_l[:, c, :])], "N")

            def gate_or_up(g, at, dst, name):
                eng.wait_ge(S["zTl"], PAIRS * (g + 1))
                if g == 0 and at == 0:
                    eng.wait_ge(S["w_gul"], 2)
                w = slice(at, at + P)
                products(dst[:, :], [
                    pair for k in range(DC)
                    for pair in parts3(wgu_h[:, k, w], wgu_l[:, k, w], zT_h[:, k, :], zT_l[:, k, :])], name)

            def G(g, c, dst):
                gate_or_up(g, c * P, dst, "G")

            def U(g, c, dst):
                gate_or_up(g, (HF + c) * P, dst, "G")

            def GU(g, c, dst):
                gate_or_up(g, 2 * HF * P, dst, "GU")

            def Dn(g, c):
                eng.wait_ge(S["hl"], HC * g + c + 1)
                if c == 0:
                    eng.wait_ge(S["r2"], TILES * g)
                    if g == 0:
                        eng.wait_ge(S["w_dl"], 3)
                slot = (HF * g + c) % HRING
                for t in range(TILES):
                    s = slice(t * P, (t + 1) * P)
                    if c < HF:
                        pairs = parts3(h_h[:, slot, s], h_l[:, slot, s], wd_h[:, c, :], wd_l[:, c, :])
                    else:
                        pairs = ((ht[:, s], wd_h[:, c, :]), (ht[:, s], wd_l[:, c, :]))
                    products(d_bank[t // 2][:, (t % 2) * D:(t % 2 + 1) * D],
                             pairs, "D" if t == TILES - 1 else None, first=c == 0 and t % 2 == 0,
                             last=c == HC - 1, skip_group_check=True)

            def setup_sums():
                eng.wait_ge(S["w_abs"], 1)
                eng.matmul(d_bank[0][:, 0:1], ones[:, :], tscale[:, 2:3], start=True, stop=True)\
                   .then_inc(S["w_sum"], 1)

            def setup_biases():
                eng.wait_ge(s_w["gu"], 16 * 4)
                for a in range(2):
                    for c in range(HC):
                        at = a * HC + c
                        src = (raw_gu[:, :, (a * HF + c) * P:(a * HF + c + 1) * P] if c < HF
                               else raw_tail[:, :, a * UT:a * UT + HT])
                        for k in range(DC):
                            ins = eng.matmul(d_bank[0][0:P if c < HF else HT, at:at + 1], src[:, k, :],
                                             b1c[:, k:k + 1], start=k == 0, stop=k == DC - 1)
                ins.then_inc(S["w_hb0"], 1)

            def setup_transposes():
                eng.wait_ge(S["w_tern"], 1)
                for k in range(DC):
                    for o in range(DC):
                        ins = eng.transpose(d_bank[1][:, k * D + o * P:k * D + (o + 1) * P],
                                            raw_t[:, o, k * P:(k + 1) * P], ident[:, :])
                ins.then_inc(S["w_ternT"], 1)

            run = {"TX": TX, "TZ": TZ, "K": K, "B": B, "Q": Q, "KV": KV, "N": N, "G": G, "U": U, "GU": GU}
            eng.wait_ge(s_cst, 8)
            for i in ITERATIONS:
                for kind, g, n in schedule(i):
                    if kind == "XK":
                        XK(g, n)
                    elif kind == "D":
                        Dn(g, n)
                    else:
                        number = NUMBER[kind, g, n]
                        if number >= RING:
                            stage_, count = freed(*JOBS[number - RING])
                            eng.wait_ge(S[stage_], count)
                        run[kind](g, n, bank[number % RING])
                if i == -LEAD:
                    eng.wait_ge(s_vec, 16 * VECTORS)
                    setup_biases()
                if i == 1 - LEAD:
                    eng.wait_ge(S["w_hb"], 2)
                    setup_sums()
                if i == 2 - LEAD:
                    setup_transposes()


_INS = ["L0_attn_x", "L0_attn_Wqkv", "L0_attn_bqkv", "L0_attn_Wg", "L0_attn_bg", "L0_attn_Wu", "L0_attn_bu",
        "L0_attn_Wd", "L0_attn_bd", "L0_attn_g1", "L0_attn_b1", "L0_attn_g2", "L0_attn_b2", "L0_ffn_weight"]
_OUT = (BATCH, SEQ, D)


def kernel(**inputs):
    import numpy as _np
    import concourse.bacc as _bacc
    from concourse import mybir as _mybir
    from concourse.bass_utils import run_bass_kernel_spmd as _run

    nc = _bacc.Bacc("TRN2", target_bir_lowering=False, num_devices=1)
    arrays, args = {}, []
    for name in _INS:
        a = _np.ascontiguousarray(inputs[name])
        arrays[f"in_{name}_dram"] = a
        args.append(nc.dram_tensor(f"in_{name}_dram", a.shape, _mybir.dt.from_np(a.dtype), kind="ExternalInput").ap())
    args.append(nc.dram_tensor("out_dram", _OUT, _mybir.dt.float32, kind="ExternalOutput").ap())
    build_kernel(nc, *args)
    r = _run(nc, [arrays], core_ids=[0])
    return r.results[0]["out_dram"]
```

```python
from contextlib import ExitStack

import concourse.bass as bass
from concourse import mybir

P = 128
D = 256
DC = D // P
H = 682
HF = H // P
HT = H - HF * P
HC = HF + 1
UT = 64
BATCH, SEQ = 8, 2048
TOK = 512
TILES = TOK // P
PAIRS = TILES // 2
GROUPS = BATCH * SEQ // TOK
GPB = SEQ // TOK
LEAD = GPB + 1
KVW = D + 2
LN_EPS = 1e-5
ATTN_EPS = 1e-6
SCALE_EPS = 1e-5
RING = 5
HRING = 3
KP = 4
SG = 3
RZ = 3
LN0 = LEAD + 1
FIRST_WARM = 3
WARM_PRODUCTS = 3
POOL_LAST = 2
XT = LEAD


def steps(text):
    return [(name, int(n)) for name, n in (step.split() for step in text.split(","))]


LATE_D = 4
TENSOR_JOBS = steps("""
    Q 0, K 0, D 4, Q 1, KV 0, K 1, KV 1, D 5, K 2, K 3, G 0, U 0, G 1, U 1, G 2, B 0, N 0, N 1, U 2,
    N 2, B 1, N 3, G 3, D 0, U 3, G 4, XK 0, TX 0, U 4, XK 1, TX 1, XK 2, XK 3, GU 5, D 1, D 2,
    TZ 0, D 3, TZ 1""")
SCALAR_STEPS = steps("""
    zT_high 0, zT_high 1, xk_copy 0, q_exp 0, q_exp 1, q_high 0, kv_high 0, k_exp 0, kv_high 1,
    k_exp 1, q_high 1, k_exp 2, silu_gate 0, x_res 0, silu_gate 1, h_high 0, k_high 0, x_res 1,
    silu_gate 2, silu_tern 0, h_high 1, x_res 2, k_exp 3, k_high 1, x_res 3, k_high 2, silu_tern 1,
    silu_gate 3, k_high 3, xT_high 0, h_high 2, silu_gate 4, xT_high 1, z_rows 0, z_rows 1,
    h_high 3, z_rows 2, z_rows 3, h_high 4, xn_high 0, silu_gate 5, xn_high 1, h_high 5""")
VECTOR_STEPS = steps("""
    a_stats 0, zT_low 0, zT_low 1, q_elu 0, kv_bias 0, k_add 0, k_add 1, q_elu 1, kv_bias 1,
    kv_low 0, k_add 2, k_max 0, ffn_rows 0, k_max 1, kv_low 1, ffn_rows 1, q_low 0, ffn_rows 2,
    ffn_rows 3, q_low 1, k_add 3, last_stats 0, h_rows 0, h_rows 1, h_low 0, attn 0, attn 1,
    k_low 0, h_low 1, k_max 2, h_rows 2, a_norm 0, attn 2, k_low 1, attn 3, q_aggregate 0, k_max 3,
    k_low 2, k_low 3, h_low 2, h_rows 3, attn_norm 0, last_norm 0, h_rows 4, last_norm 1,
    last_result 2, h_low 3, last_result 3, xT_low 0, h_low 4, h_rows 5, xT_low 1, h_low 5""")
GPSIMD_STEPS = steps("""
    xn_low 0, z_g1 0, last_rstd 0, xn_low 1, z_g1 1, sum_k 0, a_rstd 0, q_rstd 0, result 0, sum_k 1,
    z_g1 2, sum_k 2, result 1, result 2, result 3, sum_k 3, z_g1 3""")
FILL_JOBS = steps("""
    K 0, K 1, setup_bias_0 1, setup_bias_1 1, K 2, setup_bias_2 2, K 3, warm 0, warm 1, XK 0,
    setup_transposes 3, TX 0, TX 1, XK 1, XK 2, setup_sum 1, XK 3""")
FILL_SCALAR = steps("""
    setup_row_0 1, setup_abs 0, k_exp 0, k_exp 1, k_high 0, setup_d_high 2, setup_row_2 2, k_exp 2,
    k_exp 3, k_high 1, k_high 2, xT_high 0, k_high 3, xT_high 1, setup_gu_high_1 3, setup_row_1 1,
    setup_gu_high_0 0, xn_high 0, setup_q_high 0, xn_high 1""")
FILL_VECTOR = steps("""
    a_stats 0, k_add 0, k_add 1, k_add 2, k_max 0, setup_gu_low_0 2, setup_ternary 3, setup_bq 2,
    k_add 3, k_low 0, k_max 1, a_norm 0, k_max 2, k_max 3, k_low 1, k_low 2, xT_low 0, k_low 3,
    xT_low 1, setup_q_low 0, setup_ternary_parts 3, setup_gu_low_1 3""")
FILL_GPSIMD = steps("""
    xn_low 0, a_rstd 0, xn_low 1, sum_k 0, sum_k 1, sum_k 2, setup_d_low 2, sum_k 3""")


def filling(i):
    return i + 1 < 0


def schedule(i):
    a, q, f = i + LEAD, i + 1, i
    jobs = []

    def add(kind, g, n):
        if 0 <= g < GROUPS or kind == "warm":
            jobs.append((kind, g, n))

    if a == 0:
        for n in range(FIRST_WARM):
            add("warm", -1, n)
        add("TX", 0, 0)
        add("TX", 0, 1)
    for kind, n in FILL_JOBS if filling(i) else TENSOR_JOBS:
        if kind.startswith("setup_"):
            if n == a:
                add(kind, a, 0)
        elif kind != "KV" or q % GPB == 0:
            add(kind, {"K": a, "warm": a, "XK": a, "TX": a + 1, "G": f, "U": f, "GU": f,
                       "D": f - 1 if n >= LATE_D else f}.get(kind, q), n)
    return jobs


VECTORS = 11
ITERATIONS = range(-LEAD, GROUPS + 1)
SETUP_JOBS = ("setup_bias_0", "setup_bias_1", "setup_bias_2", "setup_sum", "setup_transposes")
OWN_BANK = ("D", "XK")
JOBS = [j for i in ITERATIONS for j in schedule(i) if j[0] not in OWN_BANK + SETUP_JOBS]
WARMS = [j for j in JOBS if j[0] == "warm"]
NUMBER = {j: n for n, j in enumerate(JOBS)}


def build_kernel(nc, x, wqkv, bqkv, wg, bg, wu, bu, wd, bd, g1, b1, g2, b2, wt, out):
    f32, f32r = mybir.dt.float32, mybir.dt.float32r
    ALU, ACT = mybir.AluOpType, mybir.ActivationFunctionType

    x_v = x.rearrange("b s d -> (b s) d").rearrange("(g t p) d -> g p t d", t=TILES, p=P)
    out_v = out.rearrange("b s d -> (b s) d").rearrange("(g t p) d -> g p t d", t=TILES, p=P)

    def row(v):
        return v.rearrange("(a n) -> a n", a=1)

    ctx = ExitStack()
    with ctx:
        def sb(name, shape, dt=f32):
            return ctx.enter_context(nc.sbuf_tensor(name, shape, dt))

        def sem(name):
            return ctx.enter_context(nc.semaphore(name))

        ident = sb("ident", [P, P])
        ones = sb("ones", [P, P])
        one_zero = sb("one_zero", [P, 2])
        neg_half = sb("neg_half", [P, 1])
        wqk_h = sb("wqk_h", [P, DC, 2 * D], f32r)
        wqk_l = sb("wqk_l", [P, DC, 2 * D], f32r)
        tern = sb("tern", [P, DC, D], f32r)
        NGU = (2 * HF + 1) * P
        wgu_h = sb("wgu_h", [P, DC, NGU], f32r)
        wgu_l = sb("wgu_l", [P, DC, NGU], f32r)
        wd_h = sb("wd_h", [P, HC, D], f32r)
        wd_l = sb("wd_l", [P, HC, D], f32r)
        wv = sb("wv", [P, DC, D])
        bvb = sb("bvb", [P, D])
        bk1b = sb("bk1b", [P, D])
        bq = sb("bq", [P, DC])
        bq1 = sb("bq1", [P, DC])
        nbq = sb("nbq", [P, DC])
        g1c = sb("g1c", [P, DC])
        b1c = sb("b1c", [P, DC])
        hb = sb("hb", [P, 2 * HC])
        hb0 = sb("hb0", [P, 2 * HC])
        hb1 = sb("hb1", [P, 2 * HC])
        tscale = sb("tscale", [P, 4])
        g1b = sb("g1b", [P, D])
        g2b = sb("g2b", [P, D])
        b2b = sb("b2b", [P, D])
        xa = sb("xa", [P, 2, TILES, D])
        xn = sb("xn", [P, TILES, D])
        xn_h = sb("xn_h", [P, TILES, D], f32r)
        xn_l = sb("xn_l", [P, TILES, D], f32r)
        xT_h = sb("xT_h", [P, XT, DC, TOK], f32r)
        xT_l = sb("xT_l", [P, XT, DC, TOK], f32r)
        st = sb("st", [P, 3, TILES, 6])
        mv = sb("mv", [P, 3, TILES, 2])
        ve = sb("ve", [P, 3, TILES])
        rstd0 = sb("rstd0", [P, LN0, TILES])
        nmr0 = sb("nmr0", [P, LN0, TILES])
        kp = sb("kp", [P, KP, D])
        ku = sb("ku", [P, 2, D])
        kp_h = sb("kp_h", [P, TILES, D], f32r)
        kp_l = sb("kp_l", [P, TILES, D], f32r)
        ksum = sb("ksum", [P, 2, D])
        kv_h = sb("kv_h", [P, DC, KVW], f32r)
        kv_l = sb("kv_l", [P, DC, KVW], f32r)
        xq = sb("xq", [P, 3, TILES, D])
        qp = sb("qp", [P, DC, TOK])
        qp_h = sb("qp_h", [P, DC, TOK], f32r)
        qp_l = sb("qp_l", [P, DC, TOK], f32r)
        den = sb("den", [P, 2, 2])
        rstd1 = sb("rstd1", [P, TILES])
        nmr1 = sb("nmr1", [P, TILES])
        rz = sb("rz", [P, RZ, TILES, D])
        zT_h = sb("zT_h", [P, DC, TOK], f32r)
        zT_l = sb("zT_l", [P, DC, TOK], f32r)
        sg = sb("sg", [P, SG, TILES, D])
        hs = sb("hs", [P, 2, TOK])
        h_h = sb("h_h", [P, HRING, TOK], f32r)
        h_l = sb("h_l", [P, HRING, TOK], f32r)
        ht = sb("ht", [P, TOK], f32r)
        rstd2 = sb("rstd2", [P, TILES])

        bank = [ctx.enter_context(nc.psum_tensor(f"bank{n}", [P, 512], f32)) for n in range(RING)]
        xk_bank = ctx.enter_context(nc.psum_tensor("xk_bank", [P, 512], f32))
        d_bank = [ctx.enter_context(nc.psum_tensor(f"d_bank{n}", [P, 512], f32)) for n in range(2)]

        s_w = {n: sem("s_load_" + n) for n in ("qk", "t", "bk", "gu", "d", "v")}
        s_clear = sem("s_clear")
        s_vec = sem("s_vec")
        s_b1w = sem("s_b1w")
        s_hb1 = sem("s_hb1")
        s_xa = [sem(f"s_xa{n}") for n in range(2)]
        s_xq = [sem(f"s_xq{n}") for n in range(3)]
        s_out = [sem(f"s_out{n}") for n in range(RZ)]
        s_out_rest = sem("s_out_rest")
        s_cst = sem("s_cst")
        names = ("warm w_bq1 w_bk w_qkh w_qkl w_abs w_sum w_scale w_half "
                 "w_neg w_tern w_ternT w_tern_r w_b1w w_row w_hb w_guh w_gul w_dh w_dl w_dt "
                 "bn0 ag0 ve0 rs0 xn nm0 xh xl TX xTh xTl K k1 mK eK kp kph kpl ks XK xk KV kv kvh kvl "
                 "Q mQ eQ qp qph qpl N d1 d2 xr r bn1 ag1 ve1 rs1 nm1 z TZ zTh zTl zg B sg "
                 "G GU S h hh hl D r2 bn2 ag2 ve2 rs2 a b c o c_last o_last").split()
        S = {n: sem("s_" + n) for n in names}

        def parts3(hi_l, lo_l, hi_r, lo_r):
            return ((hi_l, hi_r), (lo_l, hi_r), (hi_l, lo_r))

        def job_bank(kind, g, n):
            return bank[NUMBER[kind, g, n] % RING]

        def freed(kind, g, n):
            return {
                "TX": ("xTl", PAIRS * g + n + 1), "K": ("k1", TILES * g + n + 1),
                "Q": ("qp", DC * g + n + 1), "KV": ("kvl", DC * (g // GPB) + n + 1),
                "N": ("r", TILES * g + n + 1), "TZ": ("zTl", PAIRS * g + n + 1),
                "B": ("sg", PAIRS * g + n + 1), "G": ("S", HC * g + n + 1),
                "warm": ("warm", WARMS.index((kind, g, n)) + 1 if kind == "warm" else 0),
                "U": ("h", HC * g + n + 1), "GU": ("h", HC * g + n + 1),
            }[kind]

        bias_line = xq[:, 1:3, :, :].rearrange("p a t d -> p (a t d)")[0:1, 0:NGU]
        b1w = nc.dram_tensor("b1w", (NGU,), f32, kind="Internal").ap()
        ROW_PARTS = [slice(at, min(at + 512, NGU)) for at in range(0, NGU, 512)]

        block = ctx.enter_context(nc.Block())

        xk = hs[:, 0, :].rearrange("p (c n) -> p c n", c=DC)
        raw_qk = qp
        raw_t = hs
        rz_row = rz[:, :, :, :].rearrange("p a t d -> p (a t d)")
        raw_all = rz_row[:, 0:DC * NGU].rearrange("p (c n) -> p c n", c=DC)
        raw_gu, raw_tail = raw_all[:, :, 0:2 * HF * P], raw_all[:, :, 2 * HF * P:NGU]
        raw_d = sg[:, :, :, :].rearrange("p a t d -> p (a t) d")

        def run_steps(order, table):
            for name, n in order:
                g, step = table[name]
                if name.startswith("setup_"):
                    if g == n:
                        step()
                elif 0 <= g < GROUPS:
                    step(g, n)

        def result(eng, g, t, c, o):
            n, row_ = TILES * g + t, rz[:, g % RZ, t, :]
            eng.wait_ge(S["b"], n + 1)
            eng.wait_ge(S["sg"], PAIRS * g + t // 2 + 1)
            eng.tensor_tensor(row_, row_, sg[:, g % SG, t, :], ALU.mult).then_inc(c[0], 1)
            eng.wait_ge(*c)
            eng.tensor_tensor(row_, row_, xq[:, g % 3, t, :], ALU.add).then_inc(o, 1)

        @block.sync
        def _(eng):
            def load_xa(g):
                if g >= 2:
                    eng.wait_ge(S["xn"], TILES * (g - 1))
                eng.dma_start(xa[:, g % 2, :, :], x_v[g]).then_inc(s_xa[g % 2], 16)

            def load_xq(g):
                if g >= 3:
                    eng.wait_ge(S["o"], TILES * (g - 2))
                eng.dma_start(xq[:, g % 3, :, :], x_v[g]).then_inc(s_xq[g % 3], 16)

            def rows(v):
                return v.rearrange("(c p) n -> p c n", p=P)

            load_xa(0)
            eng.dma_start(raw_qk[:, :, :], rows(wqkv[:, 0:2 * D])).then_inc(s_w["qk"], 16)
            eng.dma_start(raw_t[:, :, 0:D], rows(wt)).then_inc(s_w["t"], 16)
            eng.dma_start(bk1b[:, :], row(bqkv[D:2 * D]).to_broadcast([P, D])).then_inc(s_w["bk"], 16)
            load_xa(1)
            eng.wait_ge(s_clear, 3)
            for dst, v in ((bvb[:, :], bqkv[2 * D:3 * D]), (g1b[:, :], g1), (g2b[:, :], g2), (b2b[:, :], b2)):
                eng.dma_start(dst, row(v).to_broadcast([P, D])).then_inc(s_vec, 16)
            with nc.allow_non_contiguous_dma(reason="a few vectors as columns"):
                for dst, v in ((bq[:, :], bqkv[0:D]), (g1c[:, :], g1), (b1c[:, :], b1)):
                    eng.dma_start(dst, v.rearrange("(c p) -> p c", p=P)).then_inc(s_vec, 16)
                for at, v in ((0, bg), (HC, bu)):
                    eng.dma_start(hb0[:, at:at + HF], v[0:HF * P].rearrange("(c p) -> p c", p=P)).then_inc(s_vec, 16)
                    eng.dma_start(hb0[0:HT, at + HF:at + HC],
                                  v[HF * P:H].rearrange("(c p) -> p c", c=1)).then_inc(s_vec, 16)
            eng.dma_start(raw_gu[:, :, 0:HF * P], rows(wg[:, 0:HF * P])).then_inc(s_w["gu"], 16)
            eng.dma_start(raw_gu[:, :, HF * P:2 * HF * P], rows(wu[:, 0:HF * P])).then_inc(s_w["gu"], 16)
            eng.dma_start(raw_tail[:, :, 0:HT], rows(wg[:, HF * P:H])).then_inc(s_w["gu"], 16)
            eng.dma_start(raw_tail[:, :, UT:UT + HT], rows(wu[:, HF * P:H])).then_inc(s_w["gu"], 16)
            eng.dma_start(raw_d[:, 0:HF, :], rows(wd[0:HF * P, :])).then_inc(s_w["d"], 16)
            for at in (0, UT):
                eng.dma_start(raw_d[at:at + HT, HF, :], wd[HF * P:H, :]).then_inc(s_w["d"], 16)
            eng.dma_start(raw_d[HT:HT + 1, HF, :], row(bd)).then_inc(s_w["d"], 16)
            eng.dma_start(raw_d[HT + 1:HT + 2, HF, :], row(b1)).then_inc(s_w["d"], 16)
            eng.dma_start(wv[:, :, :], rows(wqkv[:, 2 * D:3 * D])).then_inc(s_w["v"], 16)
            load_xq(0)

            for i in ITERATIONS:
                a, q, last = i + LEAD, i + 1, i - 1
                if i == -1:
                    eng.wait_ge(S["w_row"], len(ROW_PARTS))
                    eng.dma_start(row(b1w), bias_line).then_inc(s_b1w, 16)
                    eng.wait_ge(s_b1w, 16)
                    load_xq(1)
                    load_xq(2)
                    with nc.allow_non_contiguous_dma(reason="a few vectors as columns"):
                        for n, tail in ((0, 0), (1, UT)):
                            eng.dma_start(hb1[:, n * HC:n * HC + HF],
                                          b1w[n * HF * P:(n + 1) * HF * P].rearrange("(c p) -> p c", p=P))\
                               .then_inc(s_hb1, 16)
                            at = 2 * HF * P + tail
                            eng.dma_start(hb1[0:HT, n * HC + HF:(n + 1) * HC],
                                          b1w[at:at + HT].rearrange("(c p) -> p c", p=HT)).then_inc(s_hb1, 16)
                if a + 2 < GROUPS:
                    load_xa(a + 2)
                if 0 <= last < GROUPS:
                    tiles = TILES if last < GROUPS - 1 else POOL_LAST
                    eng.wait_ge(S["o"], TILES * last + tiles)
                    eng.dma_start(out_v[last][:, 0:tiles, :], rz[:, last % RZ, 0:tiles, :])\
                       .then_inc(s_out[last % RZ], 16)
                if 3 <= q + 1 < GROUPS:
                    load_xq(q + 1)
            eng.wait_ge(S["o_last"], TILES - POOL_LAST)
            eng.dma_start(out_v[last][:, POOL_LAST:TILES, :], rz[:, last % RZ, POOL_LAST:TILES, :])\
               .then_inc(s_out_rest, 16)
            for n in range(RZ):
                eng.wait_ge(s_out[n], 16 * len(range(n, GROUPS, RZ)))
            eng.wait_ge(s_out_rest, 16)

        @block.gpsimd
        def _(eng):
            eng.memset(hb0[:, :], 0.0).then_inc(s_clear, 1)
            eng.memset(raw_tail, 0.0).then_inc(s_clear, 1)
            eng.memset(raw_d[:, HF, :], 0.0).then_inc(s_clear, 1)
            eng.memset(ident[:, :], 0.0).then_inc(s_cst, 1)
            eng.memset(ones[:, :], 1.0).then_inc(s_cst, 1)
            eng.memset(neg_half[:, :], -0.5).then_inc(s_cst, 1)
            eng.memset(one_zero[:, 0:1], 1.0).then_inc(s_cst, 1)
            eng.memset(one_zero[:, 1:2], 0.0).then_inc(s_cst, 1)
            eng.memset(ht[:, :].bitcast(f32), 1.0).then_inc(s_cst, 1)
            eng.wait_ge(s_cst, 6)
            eng.affine_select(out=ident[:, :], in_=ident[:, :], compare_op=ALU.not_equal, fill=1.0,
                              base=0, pattern=[[-1, P]], channel_multiplier=1).then_inc(s_cst, 1)

            def rstd(k, g, dst):
                eng.wait_ge(S[f"ve{k}"], g + 1)
                if k == 0 and g >= LN0:
                    eng.wait_ge(S["xr"], TILES * (g - LN0 + 1))
                if k == 1:
                    eng.wait_ge(S["z"], TILES * g)
                if k == 2:
                    eng.wait_ge(S["b"], TILES * g)
                eng.tensor_tensor(dst, ve[:, k, :], neg_half[:, 0:1].to_broadcast([P, TILES]),
                                  ALU.pow).then_inc(S[f"rs{k}"], 1)

            def xn_low(g, p):
                eng.wait_ge(S["xh"], PAIRS * g + p + 1)
                if g:
                    eng.wait_ge(S["XK"], TILES * g)
                t = slice(2 * p, 2 * p + 2)
                eng.tensor_tensor(xn_l[:, t, :], xn[:, t, :], xn_h[:, t, :].bitcast(f32),
                                  ALU.subtract).then_inc(S["xl"], 1)

            def sum_k(g, t):
                n, slot = TILES * g + t, (g // GPB) % 2
                eng.wait_ge(S["kp"], n + 1)
                if g % GPB == 0 and t == 0:
                    if g >= 2 * GPB:
                        eng.wait_ge(S["KV"], DC * (g // GPB - 1))
                    eng.tensor_copy(ksum[:, slot, :], kp[:, n % KP, :]).then_inc(S["ks"], 1)
                else:
                    eng.wait_ge(S["ks"], n)
                    eng.tensor_tensor(ksum[:, slot, :], ksum[:, slot, :], kp[:, n % KP, :],
                                      ALU.add).then_inc(S["ks"], 1)

            def pool_result(g, t):
                if g < GROUPS - 1 or t < POOL_LAST:
                    result(eng, g, t, (S["c"], TILES * g + t + 1), S["o"])

            def z_g1(g, t):
                row_ = rz[:, g % RZ, t, :]
                eng.wait_ge(S["TZ"], PAIRS * g + t // 2 + 1)
                if g == 0:
                    eng.wait_ge(s_vec, 16 * VECTORS)
                eng.tensor_tensor(row_, row_, g1b[:, :], ALU.mult).then_inc(S["zg"], 1)

            def setup_d_low():
                eng.wait_ge(S["w_dh"], 1)
                eng.tensor_tensor(wd_l[:, 0:HF, :], raw_d[:, 0:HF, :], wd_h[:, 0:HF, :].bitcast(f32),
                                  ALU.subtract).then_inc(S["w_dl"], 1)

            rstd(0, 0, rstd0[:, 0, :])
            for i in ITERATIONS:
                a, q, f, last = i + LEAD, i + 1, i, i - 1
                run_steps(FILL_GPSIMD if filling(i) else GPSIMD_STEPS, {
                    "xn_low": (a, xn_low), "sum_k": (a, sum_k), "z_g1": (f, z_g1), "result": (last, pool_result),
                    "a_rstd": (a + 1, lambda g, _: rstd(0, g, rstd0[:, g % LN0, :])),
                    "q_rstd": (q, lambda g, _: rstd(1, g, rstd1[:, :])),
                    "last_rstd": (last, lambda g, _: rstd(2, g, rstd2[:, :])), "setup_d_low": (a, setup_d_low)})

        @block.scalar
        def _(eng):
            def act(out_, in_, func, name, **kw):
                return eng.activation(out_, in_, func, **kw).then_inc(S[name], 1)

            def xn_high(g, p):
                t = slice(2 * p, 2 * p + 2)
                eng.wait_ge(S["xn"], TILES * g + 2 * p + 2)
                if g:
                    eng.wait_ge(S["XK"], TILES * g)
                act(xn_h[:, t, :], xn[:, t, :], ACT.Copy, "xh")

            def xT_high(g, p):
                eng.wait_ge(S["TX"], PAIRS * g + p + 1)
                if g >= XT and p == 0:
                    eng.wait_ge(S["B"], PAIRS * (g - XT + 1))
                act(xT_h[:, g % XT, :, p * D:(p + 1) * D],
                    job_bank("TX", g, p)[:, :].rearrange("p (c n) -> p c n", c=DC), ACT.Copy, "xTh")

            def k_exp(g, t):
                n = TILES * g + t
                eng.wait_ge(S["k1"], n + 1)
                if n >= 2:
                    eng.wait_ge(S["kp"], n - 1)
                act(ku[:, n % 2, :], kp[:, n % KP, :], ACT.Relu, "mK", scale=-1.0, bias=ones[:, 0:1])
                eng.wait_ge(S["mK"], n + 1)
                act(ku[:, n % 2, :], ku[:, n % 2, :], ACT.Exp, "eK", scale=-1.0)

            def k_high(g, t):
                n = TILES * g + t
                eng.wait_ge(S["kp"], n + 1)
                if g:
                    eng.wait_ge(S["XK"], TILES * (g - 1) + t + 1)
                act(kp_h[:, t, :], kp[:, n % KP, :], ACT.Copy, "kph")

            def q_exp(g, c):
                eng.wait_ge(S["Q"], DC * g + c + 1)
                if g:
                    eng.wait_ge(S["qpl"], DC * (g - 1) + c + 1)
                if g == 0:
                    eng.wait_ge(S["w_bq1"], 2)
                act(qp[:, c, :], job_bank("Q", g, c)[:, :], ACT.Relu, "mQ", scale=-1.0, bias=nbq[:, c:c + 1])
                eng.wait_ge(S["mQ"], DC * g + c + 1)
                act(qp[:, c, :], qp[:, c, :], ACT.Exp, "eQ", scale=-1.0)

            def q_high(g, c):
                eng.wait_ge(S["qp"], DC * g + c + 1)
                if g:
                    eng.wait_ge(S["N"], TILES * g)
                act(qp_h[:, c, :], qp[:, c, :], ACT.Copy, "qph")

            def x_res(g, t):
                eng.wait_ge(s_xq[g % 3], 16 * (g // 3 + 1))
                eng.wait_ge(S["nm0"], g + 1)
                if g >= RZ and t == 0:
                    eng.wait_ge(s_out[g % RZ], 16 * (g // RZ))
                act(rz[:, g % RZ, t, :], xq[:, g % 3, t, :], ACT.Identity, "xr",
                    scale=rstd0[:, g % LN0, t:t + 1], bias=nmr0[:, g % LN0, t:t + 1])

            def z_rows(g, t):
                eng.wait_ge(S["nm1"], g + 1)
                act(rz[:, g % RZ, t, :], rz[:, g % RZ, t, :], ACT.Identity, "z",
                    scale=rstd1[:, t:t + 1], bias=nmr1[:, t:t + 1])

            def zT_high(g, p):
                eng.wait_ge(S["TZ"], PAIRS * g + p + 1)
                if g:
                    eng.wait_ge(S["GU"], g)
                act(zT_h[:, :, p * D:(p + 1) * D],
                    job_bank("TZ", g, p)[:, :].rearrange("p (c n) -> p c n", c=DC), ACT.Copy, "zTh")

            def silu_gate(g, c):
                n, rows = HC * g + c, P if c < HF else HT
                if c < HF:
                    eng.wait_ge(S["G"], 2 * (HF * g + c) + 1)
                    src = job_bank("G", g, c)
                else:
                    eng.wait_ge(S["GU"], g + 1)
                    src = job_bank("GU", g, c)
                if n >= 2:
                    eng.wait_ge(S["hl"], n - 1)
                if c == 0 and (g + 1) % GPB == 0 and g + 1 < GROUPS:
                    eng.wait_ge(S["KV"], DC * ((g + 1) // GPB + 1))
                act(hs[0:rows, n % 2, :], src[0:rows, :], ACT.Silu, "S", bias=hb[0:rows, c:c + 1])

            def h_high(g, c):
                n, rows = HC * g + c, P if c < HF else HT
                eng.wait_ge(S["h"], n + 1)
                if c < HF:
                    m = HF * g + c
                    if m >= HRING:
                        gb, cb = divmod(m - HRING, HF)
                        eng.wait_ge(S["D"], HC * gb + cb + 1)
                    dst = h_h[:, m % HRING, :]
                else:
                    if g:
                        eng.wait_ge(S["D"], HC * g)
                    dst = ht[0:rows, :]
                act(dst, hs[0:rows, n % 2, :], ACT.Copy, "hh")

            def xk_copy(g, _):
                if g % GPB == 0:
                    eng.wait_ge(S["XK"], TILES * (g + GPB))
                    if g == 0:
                        eng.wait_ge(S["w_ternT"], 1)
                    if g:
                        eng.wait_ge(S["KV"], DC * (g // GPB))
                        eng.wait_ge(S["hl"], HC * (g - 1))
                    act(xk, xk_bank[:, :].rearrange("p (c n) -> p c n", c=DC), ACT.Copy, "xk")

            def kv_high(g, c):
                if g % GPB == 0:
                    eng.wait_ge(S["kv"], DC * (g // GPB) + c + 1)
                    if g:
                        eng.wait_ge(S["N"], TILES * g)
                    act(kv_h[:, c, :], job_bank("KV", g, c)[:, 0:KVW], ACT.Copy, "kvh")

            def silu_tern(g, p):
                eng.wait_ge(S["B"], PAIRS * g + p + 1)
                if g == 0:
                    eng.wait_ge(S["w_dl"], 1)
                if g == 1:
                    eng.wait_ge(S["w_dt"], 2)
                if g >= SG:
                    eng.wait_ge(S["c"], TILES * (g - SG) + 2 * p + 2)
                act(sg[:, g % SG, 2 * p:2 * p + 2, :],
                    job_bank("B", g, p)[:, :].rearrange("p (t n) -> p t n", t=2),
                    ACT.Silu, "sg", scale=tscale[:, 1:2])

            def gu_high(c):
                eng.wait_ge(s_w["gu"], 16 * 4)
                eng.wait_ge(s_vec, 16 * VECTORS)
                act(wgu_h[:, c, :], raw_all[:, c, :], ACT.Copy, "w_guh", scale=g1c[:, c:c + 1])

            def setup_q_high():
                act(wqk_h[:, :, 0:D], raw_qk[:, :, 0:D], ACT.Copy, "w_qkh")

            def setup_abs():
                eng.wait_ge(s_w["t"], 16)
                act(raw_t[:, :, D:2 * D], raw_t[:, :, 0:D], ACT.Abs, "w_abs", accum_out=tscale[:, 2:3])

            def row_copy(n):
                eng.wait_ge(S["w_b1w"], n + 1)
                w = ROW_PARTS[n]
                act(bias_line[:, w], d_bank[n % 2][0:1, 0:w.stop - w.start], ACT.Copy, "w_row")

            def setup_d_high():
                eng.wait_ge(s_w["d"], 16 * 5)
                act(wd_h[:, :, :], raw_d[:, 0:HC, :], ACT.Copy, "w_dh")

            eng.wait_ge(s_w["qk"], 16)
            act(wqk_h[:, :, D:2 * D], raw_qk[:, :, D:2 * D], ACT.Copy, "w_qkh")
            xn_high(0, 0)
            xn_high(0, 1)
            xT_high(0, 0)
            xT_high(0, 1)

            for i in ITERATIONS:
                a, q, f = i + LEAD, i + 1, i
                run_steps(FILL_SCALAR if filling(i) else SCALAR_STEPS, {
                    "setup_q_high": (a, setup_q_high), "setup_abs": (a, setup_abs),
                    "setup_gu_high_0": (a, lambda: gu_high(0)), "setup_gu_high_1": (a, lambda: gu_high(1)),
                    "setup_d_high": (a, setup_d_high), "setup_row_0": (a, lambda: row_copy(0)),
                    "setup_row_1": (a, lambda: row_copy(1)), "setup_row_2": (a, lambda: row_copy(2)),
                    "zT_high": (f, zT_high), "xk_copy": (q, xk_copy), "q_exp": (q, q_exp), "k_exp": (a, k_exp),
                    "q_high": (q, q_high), "k_high": (a, k_high), "kv_high": (q, kv_high),
                    "silu_gate": (f, silu_gate), "x_res": (q, x_res), "h_high": (f, h_high),
                    "silu_tern": (q, silu_tern), "xT_high": (a + 1, xT_high), "z_rows": (q, z_rows),
                    "xn_high": (a + 1, xn_high)})

        @block.vector
        def _(eng):
            def stats(k, g, t, rows):
                n = TILES * g + t
                if n >= TILES:
                    eng.wait_ge(S[f"ag{k}"], n - TILES + 1)
                eng.bn_stats(st[:, k, t, :], rows).then_inc(S[f"bn{k}"], 1)

            def aggregate(k, g):
                for t in range(TILES):
                    eng.wait_ge(S[f"bn{k}"], TILES * g + t + 1)
                    if g and t == 0:
                        eng.wait_ge(S[{0: "nm0", 1: "nm1", 2: "a"}[k]], {0: g, 1: g, 2: TILES * g}[k])
                    eng.bn_aggr(mv[:, k, t, :], st[:, k, t, :]).then_inc(S[f"ag{k}"], 1)
                eng.wait_ge(S[f"ag{k}"], TILES * (g + 1))
                if g:
                    eng.wait_ge(S[f"rs{k}"], g)
                eng.tensor_scalar(ve[:, k, :], mv[:, k, :, 1], LN_EPS, None, ALU.add)\
                   .then_inc(S[f"ve{k}"], 1)

            def a_stats(g, _=0):
                eng.wait_ge(s_xa[g % 2], 16 * (g // 2 + 1))
                for t in range(TILES):
                    stats(0, g, t, xa[:, g % 2, t, :])
                aggregate(0, g)

            def a_norm(g, _=0):
                eng.wait_ge(S["rs0"], g + 1)
                if g:
                    eng.wait_ge(S["xl"], PAIRS * g)
                    eng.wait_ge(S["TX"], PAIRS * g)
                for t in range(TILES):
                    eng.tensor_scalar(xn[:, t, :], xa[:, g % 2, t, :], mv[:, 0, t, 0:1],
                                      rstd0[:, g % LN0, t:t + 1], ALU.subtract, ALU.mult).then_inc(S["xn"], 1)
                if g >= LN0:
                    eng.wait_ge(S["xr"], TILES * (g - LN0 + 1))
                eng.scalar_tensor_tensor(out=nmr0[:, g % LN0, :], in0=mv[:, 0, :, 0], scalar=-1.0,
                                         in1=rstd0[:, g % LN0, :], op0=ALU.mult, op1=ALU.mult).then_inc(S["nm0"], 1)

            def xT_low(g, p):
                eng.wait_ge(S["xTh"], PAIRS * g + p + 1)
                cols = slice(p * D, (p + 1) * D)
                eng.tensor_tensor(xT_l[:, g % XT, :, cols],
                                  job_bank("TX", g, p)[:, :].rearrange("p (c n) -> p c n", c=DC),
                                  xT_h[:, g % XT, :, cols].bitcast(f32), ALU.subtract).then_inc(S["xTl"], 1)

            def k_add(g, t):
                n = TILES * g + t
                eng.wait_ge(S["K"], n + 1)
                if n >= KP:
                    eng.wait_ge(S["ks"], n - KP + 1)
                eng.tensor_tensor(kp[:, n % KP, :], job_bank("K", g, t)[:, 0:D], bk1b[:, :],
                                  ALU.add).then_inc(S["k1"], 1)

            def k_max(g, t):
                n = TILES * g + t
                eng.wait_ge(S["eK"], n + 1)
                eng.tensor_tensor(kp[:, n % KP, :], kp[:, n % KP, :], ku[:, n % 2, :],
                                  ALU.max).then_inc(S["kp"], 1)

            def k_low(g, t):
                n = TILES * g + t
                eng.wait_ge(S["kph"], n + 1)
                eng.tensor_tensor(kp_l[:, t, :], kp[:, n % KP, :], kp_h[:, t, :].bitcast(f32),
                                  ALU.subtract).then_inc(S["kpl"], 1)

            def q_elu(g, c):
                n = DC * g + c
                eng.wait_ge(S["eQ"], n + 1)
                eng.scalar_tensor_tensor(out=qp[:, c, :], in0=job_bank("Q", g, c)[:, :],
                                         scalar=bq1[:, c:c + 1], in1=qp[:, c, :],
                                         op0=ALU.add, op1=ALU.max).then_inc(S["qp"], 1)

            def q_low(g, c):
                eng.wait_ge(S["qph"], DC * g + c + 1)
                eng.tensor_tensor(qp_l[:, c, :], qp[:, c, :], qp_h[:, c, :].bitcast(f32),
                                  ALU.subtract).then_inc(S["qpl"], 1)

            def attn(g, t):
                n, num = TILES * g + t, job_bank("N", g, t)
                eng.wait_ge(S["N"], n + 1)
                eng.tensor_scalar(den[:, n % 2, 0:1], num[:, D:D + 1], ATTN_EPS, None, ALU.add)\
                   .then_inc(S["d1"], 1)
                eng.wait_ge(S["d1"], n + 1)
                eng.reciprocal(den[:, n % 2, 1:2], den[:, n % 2, 0:1]).then_inc(S["d2"], 1)
                eng.wait_ge(S["d2"], n + 1)
                eng.wait_ge(S["xr"], n + 1)
                eng.scalar_tensor_tensor(out=rz[:, g % RZ, t, :], in0=num[:, 0:D],
                                         scalar=den[:, n % 2, 1:2], in1=rz[:, g % RZ, t, :],
                                         op0=ALU.mult, op1=ALU.add).then_inc(S["r"], 1)
                eng.wait_ge(S["r"], n + 1)
                stats(1, g, t, rz[:, g % RZ, t, :])

            def attn_norm(g, _=0):
                eng.wait_ge(S["rs1"], g + 1)
                if g:
                    eng.wait_ge(S["z"], TILES * g)
                eng.scalar_tensor_tensor(out=nmr1[:, :], in0=mv[:, 1, :, 0], scalar=-1.0,
                                         in1=rstd1[:, :], op0=ALU.mult, op1=ALU.mult).then_inc(S["nm1"], 1)

            def zT_low(g, p):
                eng.wait_ge(S["zTh"], PAIRS * g + p + 1)
                cols = slice(p * D, (p + 1) * D)
                eng.tensor_tensor(zT_l[:, :, cols],
                                  job_bank("TZ", g, p)[:, :].rearrange("p (c n) -> p c n", c=DC),
                                  zT_h[:, :, cols].bitcast(f32), ALU.subtract).then_inc(S["zTl"], 1)

            def h_rows(g, c):
                n, rows = HC * g + c, P if c < HF else HT
                if c < HF:
                    eng.wait_ge(S["G"], 2 * (HF * g + c + 1))
                    up = job_bank("U", g, c)[:, :]
                else:
                    up = job_bank("GU", g, c)[UT:UT + HT, :]
                eng.wait_ge(S["S"], n + 1)
                eng.scalar_tensor_tensor(out=hs[0:rows, n % 2, :], in0=up,
                                         scalar=hb[0:rows, HC + c:HC + c + 1],
                                         in1=hs[0:rows, n % 2, :], op0=ALU.add, op1=ALU.mult)\
                   .then_inc(S["h"], 1)

            def h_low(g, c):
                n, rows = HC * g + c, P if c < HF else HT
                eng.wait_ge(S["hh"], n + 1)
                hi, lo = ((h_h[:, (HF * g + c) % HRING, :], h_l[:, (HF * g + c) % HRING, :]) if c < HF
                          else (ht[0:rows, :], ht[UT:UT + rows, :]))
                eng.tensor_tensor(lo, hs[0:rows, n % 2, :], hi.bitcast(f32),
                                  ALU.subtract).then_inc(S["hl"], 1)

            def ffn_rows(g, t):
                eng.wait_ge(S["D"], HC * (g + 1))
                eng.wait_ge(S["zg"], TILES * g + t + 1)
                row_ = rz[:, g % RZ, t, :]
                eng.tensor_tensor(row_, d_bank[t // 2][:, (t % 2) * D:(t % 2 + 1) * D], row_,
                                  ALU.add).then_inc(S["r2"], 1)

            def last_stats(g, _=0):
                for t in range(TILES):
                    eng.wait_ge(S["r2"], TILES * g + t + 1)
                    stats(2, g, t, rz[:, g % RZ, t, :])
                aggregate(2, g)

            def last_norm(g, p):
                eng.wait_ge(S["rs2"], g + 1)
                pair = range(2 * p, 2 * p + 2)
                for t in pair:
                    row_ = rz[:, g % RZ, t, :]
                    eng.scalar_tensor_tensor(out=row_, in0=row_, scalar=mv[:, 2, t, 0:1], in1=g2b[:, :],
                                             op0=ALU.subtract, op1=ALU.mult).then_inc(S["a"], 1)
                for t in pair:
                    row_ = rz[:, g % RZ, t, :]
                    eng.wait_ge(S["a"], TILES * g + t + 1)
                    eng.scalar_tensor_tensor(out=row_, in0=row_, scalar=rstd2[:, t:t + 1], in1=b2b[:, :],
                                             op0=ALU.mult, op1=ALU.add).then_inc(S["b"], 1)

            def last_result(g, t):
                if g == GROUPS - 1 and t >= POOL_LAST:
                    result(eng, g, t, (S["c_last"], t - POOL_LAST + 1), S["o_last"])

            def kv_bias(g, c):
                if g % GPB == 0:
                    eng.wait_ge(S["KV"], DC * (g // GPB) + c + 1)
                    kv = job_bank("KV", g, c)
                    eng.scalar_tensor_tensor(out=kv[:, 0:D], in0=bvb[:, :], scalar=kv[:, D:D + 1],
                                             in1=kv[:, 0:D], op0=ALU.mult, op1=ALU.add).then_inc(S["kv"], 1)

            def kv_low(g, c):
                if g % GPB == 0:
                    eng.wait_ge(S["kvh"], DC * (g // GPB) + c + 1)
                    eng.tensor_tensor(kv_l[:, c, :], job_bank("KV", g, c)[:, 0:KVW],
                                      kv_h[:, c, :].bitcast(f32), ALU.subtract).then_inc(S["kvl"], 1)

            def setup_bk():
                eng.wait_ge(s_w["bk"], 16)
                eng.tensor_scalar(bk1b[:, :], bk1b[:, :], 1.0, None, ALU.add).then_inc(S["w_bk"], 1)

            def setup_qk_low(half):
                w = slice(half * D, (half + 1) * D)
                eng.wait_ge(S["w_qkh"], 2 - half)
                eng.tensor_tensor(wqk_l[:, :, w], raw_qk[:, :, w], wqk_h[:, :, w].bitcast(f32),
                                  ALU.subtract).then_inc(S["w_qkl"], 1)

            def setup_bq():
                eng.wait_ge(s_vec, 16 * VECTORS)
                eng.tensor_scalar(bq1[:, :], bq[:, :], 1.0, None, ALU.add).then_inc(S["w_bq1"], 1)
                eng.tensor_scalar(nbq[:, :], bq[:, :], -1.0, None, ALU.mult).then_inc(S["w_bq1"], 1)

            def setup_ternary():
                eng.wait_ge(S["w_sum"], 1)
                eng.tensor_scalar(tscale[:, 1:2], d_bank[1][:, 0:1], 1.0 / (D * D), SCALE_EPS,
                                  ALU.mult, ALU.max).then_inc(S["w_scale"], 1)
                eng.wait_ge(S["w_scale"], 1)
                eng.tensor_scalar(tscale[:, 0:1], tscale[:, 1:2], 0.5, None, ALU.mult)\
                   .then_inc(S["w_half"], 1)
                eng.wait_ge(S["w_half"], 1)
                eng.tensor_scalar(raw_t[:, :, D:2 * D], raw_t[:, :, 0:D], -1.0, tscale[:, 0:1],
                                  ALU.mult, ALU.is_gt).then_inc(S["w_neg"], 1)
                eng.wait_ge(S["w_neg"], 1)
                eng.scalar_tensor_tensor(out=raw_t[:, :, 0:D], in0=raw_t[:, :, 0:D], scalar=tscale[:, 0:1],
                                         in1=raw_t[:, :, D:2 * D], op0=ALU.is_gt, op1=ALU.subtract)\
                   .then_inc(S["w_tern"], 1)

            def setup_ternary_parts():
                eng.wait_ge(S["w_ternT"], 1)
                eng.tensor_copy(tern[:, :, :], d_bank[1][:, :].rearrange("p (c n) -> p c n", c=DC))\
                   .then_inc(S["w_tern_r"], 1)

            def setup_hidden_biases():
                eng.wait_ge(s_vec, 16 * VECTORS)
                eng.wait_ge(s_hb1, 16 * 4)
                eng.tensor_tensor(cols(hb)[:, :, 0:HF], cols(hb1)[:, :, 0:HF],
                                  cols(hb0)[:, :, 0:HF], ALU.add).then_inc(S["w_hb"], 1)
                eng.tensor_tensor(cols(hb)[0:HT, :, HF:HC], cols(hb1)[0:HT, :, HF:HC],
                                  cols(hb0)[0:HT, :, HF:HC], ALU.add).then_inc(S["w_hb"], 1)

            def setup_gu_low(c):
                eng.wait_ge(S["w_guh"], c + 1)
                eng.scalar_tensor_tensor(out=wgu_l[:, c, :], in0=raw_all[:, c, :], scalar=g1c[:, c:c + 1],
                                         in1=wgu_h[:, c, :].bitcast(f32), op0=ALU.mult, op1=ALU.subtract)\
                   .then_inc(S["w_gul"], 1)

            def setup_d_tail():
                eng.wait_ge(S["w_dh"], 1)
                eng.memset(wd_l[UT:P, HF, :].bitcast(f32), 0.0).then_inc(S["w_dt"], 1)
                eng.tensor_tensor(wd_l[0:UT, HF, :], raw_d[0:UT, HF, :], wd_h[0:UT, HF, :].bitcast(f32),
                                  ALU.subtract).then_inc(S["w_dt"], 1)

            def cols(t):
                return t[:, 0:2 * HC].rearrange("p (a c) -> p a c", a=2)

            a_stats(0)
            setup_bk()
            a_norm(0)
            setup_qk_low(1)
            xT_low(0, 0)
            xT_low(0, 1)

            for i in ITERATIONS:
                a, q, f, last = i + LEAD, i + 1, i, i - 1
                run_steps(FILL_VECTOR if filling(i) else VECTOR_STEPS, {
                    "setup_q_low": (a, lambda: setup_qk_low(0)), "setup_bq": (a, setup_bq),
                    "setup_gu_low_0": (a, lambda: setup_gu_low(0)), "setup_gu_low_1": (a, lambda: setup_gu_low(1)),
                    "setup_ternary": (a, setup_ternary), "setup_ternary_parts": (a, setup_ternary_parts),
                    "zT_low": (f, zT_low), "a_stats": (a + 1, a_stats), "q_elu": (q, q_elu), "k_add": (a, k_add),
                    "q_low": (q, q_low), "k_max": (a, k_max), "k_low": (a, k_low), "kv_bias": (q, kv_bias),
                    "kv_low": (q, kv_low), "ffn_rows": (last, ffn_rows),
                    "h_rows": (f, h_rows), "attn": (q, attn), "h_low": (f, h_low), "a_norm": (a + 1, a_norm),
                    "q_aggregate": (q, lambda g, _: aggregate(1, g)), "last_stats": (last, last_stats),
                    "attn_norm": (q, attn_norm), "last_norm": (last, last_norm),
                    "last_result": (last, last_result), "xT_low": (a + 1, xT_low)})
                if i == -1:
                    setup_d_tail()
                    setup_hidden_biases()

        @block.tensor
        def _(eng):
            def products(dst, pairs, name, first=True, last=True, **kw):
                for n, (left, right) in enumerate(pairs):
                    ins = eng.matmul(dst, left, right, start=first and n == 0,
                                     stop=last and n == len(pairs) - 1, **kw)
                if name:
                    ins.then_inc(S[name], 1)

            def x_parts(g, t):
                s = slice(t * P, (t + 1) * P)
                return [(xT_h[:, g % XT, c, s], xT_l[:, g % XT, c, s]) for c in range(DC)]

            def transposes(dst, src, p, name):
                for c in range(DC):
                    for t in range(2):
                        ins = eng.transpose(dst[:, c * D + t * P:c * D + (t + 1) * P],
                                            src[:, 2 * p + t, c * P:(c + 1) * P], ident[:, :])
                ins.then_inc(S[name], 1)

            def TX(g, p, dst):
                eng.wait_ge(S["xn"], TILES * g + 2 * p + 2)
                transposes(dst, xn, p, "TX")

            def TZ(g, p, dst):
                eng.wait_ge(S["z"], TILES * g + 2 * p + 2)
                transposes(dst, rz[:, g % RZ, :, :], p, "TZ")

            def K(g, t, dst):
                eng.wait_ge(S["xTl"], PAIRS * g + t // 2 + 1)
                if g == 0 and t == 0:
                    eng.wait_ge(S["w_qkl"], 1)
                w = slice(D, 2 * D)
                products(dst[:, 0:D], [
                    pair for c, (xh, xl) in enumerate(x_parts(g, t))
                    for pair in parts3(xh, xl, wqk_h[:, c, w], wqk_l[:, c, w])], "K")

            def B(g, p, dst):
                if g == 0 and p == 0:
                    eng.wait_ge(S["w_tern_r"], 1)
                for t in range(2):
                    products(dst[:, t * D:(t + 1) * D],
                             [(part, tern[:, c, :]) for c, parts in enumerate(x_parts(g, 2 * p + t))
                              for part in parts], "B" if t else None)

            def Q(g, c, dst):
                eng.wait_ge(S["xTl"], PAIRS * (g + 1))
                if g == 0:
                    eng.wait_ge(S["w_qkl"], 2)
                w = slice(c * P, (c + 1) * P)
                products(dst[:, :], [
                    pair for k in range(DC)
                    for pair in parts3(wqk_h[:, k, w], wqk_l[:, k, w],
                                       xT_h[:, g % XT, k, :], xT_l[:, g % XT, k, :])], "Q")

            def XK(g, t):
                n, of = TILES * (g % GPB) + t, TILES * GPB
                eng.wait_ge(S["kpl"], TILES * g + t + 1)
                eng.wait_ge(S["xl"], PAIRS * g + t // 2 + 1)
                if n == 0:
                    eng.wait_ge(S["xk"], g // GPB)
                for c in range(DC):
                    w = slice(c * P, (c + 1) * P)
                    products(xk_bank[:, c * D:(c + 1) * D],
                             parts3(xn_h[:, t, w], xn_l[:, t, w], kp_h[:, t, :], kp_l[:, t, :]),
                             "XK" if c == DC - 1 else None, first=n == 0 and c == 0,
                             last=n == of - 1, skip_group_check=True)

            def KV(g, c, dst):
                batch = g // GPB
                eng.wait_ge(S["xk"], batch + 1)
                eng.wait_ge(S["ks"], TILES * (g + GPB))
                if g == 0:
                    eng.wait_ge(s_w["v"], 16)
                w = slice(c * P, (c + 1) * P)
                products(dst[:, 0:D], [(xk[:, k, w], wv[:, k, :]) for k in range(DC)], None)
                products(dst[:, D:KVW], [(ksum[:, batch % 2, w], one_zero[:, :])], "KV")

            def N(g, t, dst):
                eng.wait_ge(S["qpl"], DC * (g + 1))
                eng.wait_ge(S["kvl"], DC * (g // GPB + 1))
                s = slice(t * P, (t + 1) * P)
                products(dst[:, 0:KVW], [
                    pair for c in range(DC)
                    for pair in parts3(qp_h[:, c, s], qp_l[:, c, s], kv_h[:, c, :], kv_l[:, c, :])], "N")

            def gate_or_up(g, at, dst, name):
                eng.wait_ge(S["zTl"], PAIRS * (g + 1))
                if g == 0 and at == 0:
                    eng.wait_ge(S["w_gul"], 2)
                w = slice(at, at + P)
                products(dst[:, :], [
                    pair for k in range(DC)
                    for pair in parts3(wgu_h[:, k, w], wgu_l[:, k, w], zT_h[:, k, :], zT_l[:, k, :])], name)

            def G(g, c, dst):
                gate_or_up(g, c * P, dst, "G")

            def U(g, c, dst):
                gate_or_up(g, (HF + c) * P, dst, "G")

            def GU(g, c, dst):
                gate_or_up(g, 2 * HF * P, dst, "GU")

            def Dn(g, c):
                eng.wait_ge(S["hl"], HC * g + c + 1)
                if c == 0:
                    eng.wait_ge(S["r2"], TILES * g)
                    if g == 0:
                        eng.wait_ge(S["w_dl"], 1)
                        eng.wait_ge(S["w_dt"], 2)
                slot = (HF * g + c) % HRING
                for t in range(TILES):
                    s = slice(t * P, (t + 1) * P)
                    if c < HF:
                        pairs = parts3(h_h[:, slot, s], h_l[:, slot, s], wd_h[:, c, :], wd_l[:, c, :])
                    else:
                        pairs = ((ht[:, s], wd_h[:, c, :]), (ht[:, s], wd_l[:, c, :]))
                    products(d_bank[t // 2][:, (t % 2) * D:(t % 2 + 1) * D],
                             pairs, "D" if t == TILES - 1 else None, first=c == 0 and t % 2 == 0,
                             last=c == HC - 1, skip_group_check=True)

            def bias_row(n):
                eng.wait_ge(s_w["gu"], 16 * 4)
                eng.wait_ge(s_vec, 16 * VECTORS)
                if n >= 2:
                    eng.wait_ge(S["w_row"], n - 1)
                w = ROW_PARTS[n]
                products(d_bank[n % 2][0:1, 0:w.stop - w.start],
                         [(b1c[:, k:k + 1], raw_all[:, k, w]) for k in range(DC)], "w_b1w")

            def warm(g, n, dst):
                products(dst[:, :], [(ht[:, 0:P], ht[:, :])] * WARM_PRODUCTS, "warm")

            def setup_sum():
                eng.wait_ge(S["w_abs"], 1)
                eng.wait_ge(S["w_row"], 2)
                eng.matmul(d_bank[1][:, 0:1], ones[:, :], tscale[:, 2:3], start=True, stop=True)\
                   .then_inc(S["w_sum"], 1)

            def setup_transposes():
                eng.wait_ge(S["w_tern"], 1)
                for k in range(DC):
                    for o in range(DC):
                        ins = eng.transpose(d_bank[1][:, k * D + o * P:k * D + (o + 1) * P],
                                            raw_t[:, o, k * P:(k + 1) * P], ident[:, :])
                ins.then_inc(S["w_ternT"], 1)

            run = {"TX": TX, "TZ": TZ, "K": K, "B": B, "Q": Q, "KV": KV, "N": N, "G": G, "U": U, "GU": GU,
                   "warm": warm}
            setup = {"setup_bias_0": lambda: bias_row(0), "setup_bias_1": lambda: bias_row(1),
                     "setup_bias_2": lambda: bias_row(2), "setup_sum": setup_sum,
                     "setup_transposes": setup_transposes}
            eng.wait_ge(s_cst, 7)
            for i in ITERATIONS:
                for kind, g, n in schedule(i):
                    if kind == "XK":
                        XK(g, n)
                    elif kind == "D":
                        Dn(g, n)
                    elif kind in setup:
                        setup[kind]()
                    else:
                        number = NUMBER[kind, g, n]
                        if number >= RING:
                            stage_, count = freed(*JOBS[number - RING])
                            eng.wait_ge(S[stage_], count)
                        run[kind](g, n, bank[number % RING])


_INS = ["L0_attn_x", "L0_attn_Wqkv", "L0_attn_bqkv", "L0_attn_Wg", "L0_attn_bg", "L0_attn_Wu", "L0_attn_bu",
        "L0_attn_Wd", "L0_attn_bd", "L0_attn_g1", "L0_attn_b1", "L0_attn_g2", "L0_attn_b2", "L0_ffn_weight"]
_OUT = (BATCH, SEQ, D)


def kernel(**inputs):
    import numpy as _np
    import concourse.bacc as _bacc
    from concourse import mybir as _mybir
    from concourse.bass_utils import run_bass_kernel_spmd as _run

    nc = _bacc.Bacc("TRN2", target_bir_lowering=False, num_devices=1)
    arrays, args = {}, []
    for name in _INS:
        a = _np.ascontiguousarray(inputs[name])
        arrays[f"in_{name}_dram"] = a
        args.append(nc.dram_tensor(f"in_{name}_dram", a.shape, _mybir.dt.from_np(a.dtype), kind="ExternalInput").ap())
    args.append(nc.dram_tensor("out_dram", _OUT, _mybir.dt.float32, kind="ExternalOutput").ap())
    build_kernel(nc, *args)
    r = _run(nc, [arrays], core_ids=[0])
    return r.results[0]["out_dram"]
```
